# Optimizing a Trainium2 kernel written in Bass

```python
import numpy as np
import jax
import jax.numpy as jnp

def _softmax(x, axis=-1):
    return jax.nn.softmax(x, axis=axis)

def _gelu(x):
    return jax.nn.gelu(x, approximate=True)

def _silu(x):
    return jax.nn.silu(x)

def _sigmoid(x):
    return jax.nn.sigmoid(x)

def _layernorm(x, axis=-1, eps=1e-05):
    m = jnp.mean(x, axis=axis, keepdims=True)
    v = jnp.var(x, axis=axis, keepdims=True)
    return (x - m) / jnp.sqrt(v + eps)

def _scatter_add(tgt, idx, src, axis=0):
    return tgt.at[idx].add(src)

def _segment_sum(src, seg, n):
    return jax.ops.segment_sum(src, seg, n)
kernel_name = 'mk_adaln_d1_jaxref_r8_793265'

def setup_inputs(seed: int=0):
    np.random.seed(seed)
    _w = jnp.asarray

    def _L0_attn_setup():
        import jax, jax.numpy as jnp
        import numpy as np
        key = jax.random.key(seed)
        k1, k2, k3, k4, k5 = jax.random.split(key, 5)
        B, S, D = (4, 512, 256)
        x = jax.random.normal(k1, (B, S, D), dtype=jnp.float32)
        W_in = jax.random.normal(k2, (D, D), dtype=jnp.float32) / np.sqrt(D)
        W_out = jax.random.normal(k3, (D, D), dtype=jnp.float32) / np.sqrt(D)
        decay = jax.random.normal(k4, (D,), dtype=jnp.float32) * 0.1
        bias = jax.random.normal(k5, (D,), dtype=jnp.float32) * 0.02
        return {'x': x, 'W_in': W_in, 'W_out': W_out, 'decay': decay, 'bias': bias}
    _L0_attn_in = _L0_attn_setup()

    def _L0_ffn_setup():
        import jax, jax.numpy as jnp
        import numpy as np
        B, S, D = (2, 256, 256)
        I = 128
        E = 32
        K = 4
        NS = 1
        ALPHA = 7.0

        def _clamped_swiglu(x, wg, wu, wd):
            g = jnp.clip(x @ wg.T, -ALPHA, ALPHA)
            u = jnp.clip(x @ wu.T, -ALPHA, ALPHA)
            return jax.nn.silu(g) * u @ wd.T
        key = jax.random.key(seed)
        ks = jax.random.split(key, 9)
        s = 0.02
        return {'hidden': jax.random.normal(ks[0], (B, S, D), jnp.float32), 'router_w': jax.random.normal(ks[1], (E, D), jnp.float32) * s, 'expert_bias': jax.random.normal(ks[2], (E,), jnp.float32) * s, 'gate_w': jax.random.normal(ks[3], (E, I, D), jnp.float32) * s, 'up_w': jax.random.normal(ks[4], (E, I, D), jnp.float32) * s, 'down_w': jax.random.normal(ks[5], (E, D, I), jnp.float32) * s, 'shared_gate_w': jax.random.normal(ks[6], (NS * I, D), jnp.float32) * s, 'shared_up_w': jax.random.normal(ks[7], (NS * I, D), jnp.float32) * s, 'shared_down_w': jax.random.normal(ks[8], (D, NS * I), jnp.float32) * s}
    _L0_ffn_in = _L0_ffn_setup()
    _L0_c = _w((lambda *s: np.random.randn(*s).astype(np.float32) * 0.05)(8, 256))
    _L0_wmod = _w((lambda *s: np.random.randn(*s).astype(np.float32) * 0.05)(256, 6 * 256) * 256 ** (-0.5))
    _d = {'L0_attn_x': _L0_attn_in['x'], 'L0_attn_W_in': _L0_attn_in['W_in'], 'L0_attn_W_out': _L0_attn_in['W_out'], 'L0_attn_decay': _L0_attn_in['decay'], 'L0_attn_bias': _L0_attn_in['bias'], 'L0_ffn_router_w': _L0_ffn_in['router_w'], 'L0_ffn_expert_bias': _L0_ffn_in['expert_bias'], 'L0_ffn_gate_w': _L0_ffn_in['gate_w'], 'L0_ffn_up_w': _L0_ffn_in['up_w'], 'L0_ffn_down_w': _L0_ffn_in['down_w'], 'L0_ffn_shared_gate_w': _L0_ffn_in['shared_gate_w'], 'L0_ffn_shared_up_w': _L0_ffn_in['shared_up_w'], 'L0_ffn_shared_down_w': _L0_ffn_in['shared_down_w'], 'L0_c': _L0_c, 'L0_wmod': _L0_wmod}
    _x0 = _d['L0_attn_x']
    _d['L0_attn_x'] = jax.random.normal(jax.random.fold_in(jax.random.key(seed), 1), (8, 256, 256), dtype=_x0.dtype)
    del _x0
    return _d

def reference(L0_attn_x, L0_attn_W_in, L0_attn_W_out, L0_attn_decay, L0_attn_bias, L0_ffn_router_w, L0_ffn_expert_bias, L0_ffn_gate_w, L0_ffn_up_w, L0_ffn_down_w, L0_ffn_shared_gate_w, L0_ffn_shared_up_w, L0_ffn_shared_down_w, L0_c, L0_wmod):

    def _L0_attn_ref(x, W_in, W_out, decay, bias):
        import jax, jax.numpy as jnp
        import numpy as np
        d = jax.nn.sigmoid(decay)
        projected = jnp.einsum('bsd,ed->bse', x, W_in)

        def step(state, seg_t):
            state = d * state + (1.0 - d) * seg_t
            return (state, state)
        init = jnp.zeros((x.shape[0], x.shape[2]), dtype=x.dtype)
        _, states = jax.lax.scan(step, init, jnp.swapaxes(projected, 0, 1))
        stacked = jnp.swapaxes(states, 0, 1)
        return jnp.einsum('bsd,ed->bse', stacked, W_out) + bias[None, None, :]

    def _L0_ffn_ref(hidden, router_w, expert_bias, gate_w, up_w, down_w, shared_gate_w, shared_up_w, shared_down_w):
        import jax, jax.numpy as jnp
        import numpy as np
        B, S, D = (2, 256, 256)
        I = 128
        E = 32
        K = 4
        NS = 1
        ALPHA = 7.0

        def _clamped_swiglu(x, wg, wu, wd):
            g = jnp.clip(x @ wg.T, -ALPHA, ALPHA)
            u = jnp.clip(x @ wu.T, -ALPHA, ALPHA)
            return jax.nn.silu(g) * u @ wd.T
        Bb, Ss, Dd = hidden.shape
        flat = hidden.reshape(-1, Dd)
        T = flat.shape[0]
        logits = flat @ router_w.T
        scores = jnp.sqrt(jax.nn.softplus(logits))
        _, idx = jax.lax.top_k(scores + expert_bias, K)
        topv = jnp.take_along_axis(scores, idx, axis=1)
        topv = topv / (topv.sum(axis=-1, keepdims=True) + 1e-20)
        probs = jnp.zeros((T, E), flat.dtype).at[jnp.arange(T)[:, None], idx].set(topv)

        def body(acc, xs):
            wg, wu, wd, p = xs
            return (acc + p[:, None] * _clamped_swiglu(flat, wg, wu, wd), None)
        out, _ = jax.lax.scan(body, jnp.zeros_like(flat), (gate_w, up_w, down_w, probs.T))
        out = out + _clamped_swiglu(flat, shared_gate_w, shared_up_w, shared_down_w)
        return out.reshape(Bb, Ss, Dd)
    x = L0_attn_x
    mod = (_silu(L0_c) @ L0_wmod).reshape(L0_c.shape[0], 6, 1, -1)
    sa, ca, ga, sb, cb, gb = (mod[:, 0], mod[:, 1], mod[:, 2], mod[:, 3], mod[:, 4], mod[:, 5])
    ga = (2 * (ga >= 0) - 1) * jnp.maximum(jnp.abs(ga), 0.25)
    gb = (2 * (gb >= 0) - 1) * jnp.maximum(jnp.abs(gb), 0.25)
    h = _layernorm(x, axis=-1) * (1 + ca) + sa
    x = x + ga * _L0_attn_ref(h, L0_attn_W_in, L0_attn_W_out, L0_attn_decay, L0_attn_bias)
    h = _layernorm(x, axis=-1) * (1 + cb) + sb
    x = x + gb * _L0_ffn_ref(h, L0_ffn_router_w, L0_ffn_expert_bias, L0_ffn_gate_w, L0_ffn_up_w, L0_ffn_down_w, L0_ffn_shared_gate_w, L0_ffn_shared_up_w, L0_ffn_shared_down_w)
    return x

_drawn_inputs = setup_inputs


def setup_inputs(seed=0):
    import zlib

    import numpy as np

    out = dict(_drawn_inputs(seed))
    spreads = {}
    factors = {'L0_attn_decay': 8.0,
     'L0_attn_bias': 8.0,
     'L0_ffn_router_w': 8.0,
     'L0_ffn_expert_bias': 8.0,
     'L0_ffn_gate_w': 8.0,
     'L0_ffn_up_w': 8.0,
     'L0_ffn_down_w': 8.0,
     'L0_ffn_shared_gate_w': 8.0,
     'L0_ffn_shared_up_w': 8.0,
     'L0_ffn_shared_down_w': 8.0}
    for name, (base, spread) in spreads.items():
        noise = np.random.default_rng([zlib.crc32(name.encode()), seed]).standard_normal(out[name].shape)
        drawn = base * np.exp(spread * noise) if base else spread * noise
        out[name] = jnp.asarray(drawn.astype(out[name].dtype))
    for name, factor in factors.items():
        out[name] = (out[name] * factor).astype(out[name].dtype)
    return out
```

```python
from contextlib import ExitStack

import concourse.bass as bass
from concourse import mybir

fp32 = mybir.dt.float32
fp16 = mybir.dt.float16
i32 = mybir.dt.int32
u32 = mybir.dt.uint32
ALU = mybir.AluOpType
ACT = mybir.ActivationFunctionType
AX = mybir.AxisListType
ds = bass.ds

P = 128
SPLIT = 256.0
CLAMP = 7.0
EPS = 1e-5
GATE_MIN = 0.25


def at_least(engine, semaphore, value):
    if isinstance(value, int) and value <= 0:
        return
    engine.wait_ge(semaphore, value)


def adaln_block(nc, x, w_in, w_out, decay, bias, router_w, expert_bias, gate_w, up_w, down_w,
                sh_gate, sh_up, sh_down, cond, wmod, out):
    B, S, D = x.shape
    E, I, _ = gate_w.shape
    K = 4
    T = B * S
    NT = T // P
    TPB = S // P
    C = D // P
    U = 4
    RT = -(-((T * K + E * (P - 1)) // P) // U) * U
    AT = RT + NT
    NM = 6
    GA, GAB, CB, SB, GB = range(5)
    NR = 5
    PAIRS = E // 2
    PPB = PAIRS // B
    HL = 2 * D

    x_t = x.rearrange("b s d -> (b s) d").rearrange("(t p) d -> p t d", p=P)
    out_t = out.rearrange("b s d -> (b s) d").rearrange("(t p) d -> p t d", p=P)
    mod_dram = nc.dram_tensor("mod_rows_dram", (B, NR * D), fp32, kind="Internal").ap()
    hid_dram = nc.dram_tensor("hidden_dram", (T, HL), fp16, kind="Internal").ap()
    y_dram = nc.dram_tensor("expert_out_dram", (RT * P, D), fp32, kind="Internal").ap()
    shared_dram = nc.dram_tensor("shared_out_dram", (T, D), fp32, kind="Internal").ap()
    hid_t = hid_dram.rearrange("(t p) d -> p t d", p=P)
    y_t = y_dram.rearrange("(t p) d -> p t d", p=P)
    shared_t = shared_dram.rearrange("(t p) d -> p t d", p=P)

    ctx = ExitStack()
    with ctx:
        def sb(name, shape, dt):
            return ctx.enter_context(nc.sbuf_tensor(name, shape, dt))

        def sem(name):
            return ctx.enter_context(nc.semaphore(name))

        xs = sb("xs", [P, NT, D], fp32)
        wgu = sb("wgu", [P, E + 1, C, 2, 2 * I], fp16)
        wdn = sb("wdn", [P, E + 1, 2, D], fp16)
        ident = sb("ident", [P, P], fp32)
        ident16 = sb("ident16", [P, P], fp16)
        iota_i = sb("iota_i", [P, P], i32)
        iota16 = sb("iota16", [P, P], fp16)
        iota32 = sb("iota32", [P, E], fp32)
        part_i = sb("part_i", [P, 1], i32)
        part_f = sb("part_f", [P, 1], fp32)
        token_i = sb("token_i", [P, NT], i32)
        token_f = sb("token_f", [P, NT], fp32)
        before16 = sb("before16", [P, P], fp16)
        ones16 = sb("ones16", [P, P], fp16)
        eps_t = sb("eps_t", [P, 1], fp32)
        one_t = sb("one_t", [P, 1], fp32)
        ebias = sb("ebias", [P, E], fp32)
        logits = sb("logits", [P, NT, E], fp32)
        gate_b = sb("gate_b", [P, B, D], fp32)
        slot_of = sb("slot_of", [P, NT, K], i32)
        token_of = sb("token_of", [P, AT + 1], i32)
        weight = sb("weight", [P, NT, K], fp32)
        tile_expert = sb("tile_expert", [1, U + AT + 2 * U], i32)
        wmod_s = sb("wmod_s", [P, C, NM * D], fp32)
        c_s = sb("c_s", [B, D], fp32)
        cT = sb("cT", [P, C, B], fp32)
        bias8 = sb("bias8", [B, D], fp32)
        rows = sb("rows", [B, NR, D], fp32)
        small_room = sb("small_room", [P, 2, 2 * D], fp32)
        rows_a = small_room[0:B, 0, :].rearrange("b (n d) -> b n d", n=2)
        rows_b = small_room[0:B, 1, :].rearrange("b (n d) -> b n d", n=2)
        modT = sb("modT", [P, 2 * C, B], fp32)
        dec = sb("dec", [C, P], fp32)
        keep = sb("keep", [P, C], fp32)
        omk = sb("omk", [P, C], fp32)
        wa_n = sb("wa_n", [P, 2, C, D], fp32)
        wa_k = sb("wa_k", [P, C, D], fp32)
        wa_T = sb("wa_T", [P, 2, C, D], fp32)
        rt_n = sb("rt_n", [E, D], fp32)
        rt_T = sb("rt_T", [P, C, 2, E], fp16)
        nat = sb("nat", [P, 2, 3, 2, D], fp32)
        nat_sh = sb("nat_sh", [P, 3, D], fp32)
        stats = sb("stats", [P, 2, 6], fp32)
        mv1 = sb("mv1", [P, NT, 2], fp32)
        sd1 = sb("sd1", [P, NT], fp32)
        rs1 = sb("rs1", [P, NT], fp32)
        nm1 = sb("nm1", [P, NT], fp32)
        bc = sb("bc", [P, 2, 2, D], fp32)
        bc_a, bc_b = bc[:, 0, :, :], bc[:, 1, :, :]
        mix_room = sb("mix_room", [P, 6, 2 * D], fp32)
        xh, gated, xh2, h2 = (mix_room[:, n, :].rearrange("p (q d) -> p q d", q=TPB) for n in range(4))
        hT, st = (mix_room[:, n, :].rearrange("p (c t) -> p c t", c=C) for n in (4, 5))
        stats2 = sb("stats2", [P, TPB, 6], fp32)
        mv2 = sb("mv2", [P, TPB, 2], fp32)
        sd2 = sb("sd2", [P, TPB], fp32)
        rs2 = sb("rs2", [P, TPB], fp32)
        nm2 = sb("nm2", [P, TPB], fp32)
        h16 = sb("h16", [P, TPB, HL], fp16)
        h16T = sb("h16T", [P, TPB, 2 * C, P], fp16)

        room = wmod_s[:, :, :].rearrange("p c n -> p (c n)")

        def routing_room(n):
            return room[:, n * NT * E:(n + 1) * NT * E].rearrange("p (t e) -> p t e", e=E)
        r0, r1, r2, r3, r4, score = (routing_room(n) for n in range(6))
        top_v = sb("top_v", [P, NT, 8], fp32)
        top_i = sb("top_i", [P, NT, 8], u32)
        top_f = sb("top_f", [P, K, NT], fp32)
        chosen = sb("chosen", [P, K, NT, E], fp16)
        picked = sb("picked", [P, NT, E], fp16)
        tiles_i = sb("tiles_i", [P, E], i32)
        tiles_f = sb("tiles_f", [P, E], fp32)
        last_tile = sb("last_tile", [P, E], fp32)
        first_tile = sb("first_tile", [P, E], fp32)
        slot_f = sb("slot_f", [P, K, NT], fp32)
        slot_tmp = sb("slot_tmp", [P, NT, K], i32)
        slot_tile = sb("slot_tile", [P, NT, K], fp32)
        slot_row = sb("slot_row", [P, NT, K], fp32)
        prob = sb("prob", [P, K, NT], fp32)
        prob_sum = sb("prob_sum", [P, NT], fp32)
        row_hot, tile_hot = (small_room[:, n, 0:K * P // 2].bitcast(fp16).rearrange("p (k r) -> p k r", k=K)
                             for n in range(2))
        te_cmp = sb("te_cmp", [P, E], fp32)
        te_col = sb("te_col", [P, 1], fp32)
        col = sb("col", [P, U], i32)
        xg = room[:, 3 * NT * E:5 * NT * E].bitcast(fp16).rearrange("p (u n) -> p u n", u=U)
        hidT = room[:, 0:NT * E].bitcast(fp16).rearrange("p (u a n) -> p u a n", u=U, a=2)
        xT = bc[:, :, :, :].rearrange("p a b d -> p (a b d)").bitcast(fp16)\
            .rearrange("p (u c t) -> p u c t", u=U, c=2 * C)
        clip = mix_room[:, 0:2, :].rearrange("p a (b n) -> p (a b) n", b=2)
        yo = mix_room[:, 2:4, :].rearrange("p a (b n) -> p (a b) n", b=2)
        act_g = mix_room[:, 4, :].rearrange("p (u n) -> p u n", u=U)
        hid = mix_room[:, 5, :].rearrange("p (u n) -> p u n", u=U)
        yg = nat[:, :, :, :, :].rearrange("p a b c d -> p (a b c) d")[:, 0:2 * (K + 1), :]\
            .rearrange("p (u k) d -> p u k d", u=2)
        col_c = sb("col_c", [P, 2, K], i32)
        acc = wa_n[:, :, :, :].rearrange("p a c d -> p (a c) d")
        fin = wa_T[:, :, :, :].rearrange("p a c d -> p (a c) d")

        bank = [ctx.enter_context(nc.psum_tensor(f"bank{n}", [P, 512], fp32)) for n in range(8)]
        bank16 = [b[:, :].bitcast(fp16) for b in bank]

        ld_cond, ld_wmod, ld_small, ld_attn, ld_shared = (
            sem(n) for n in ("ld_cond", "ld_wmod", "ld_small", "ld_attn", "ld_shared"))
        XL = 4
        ld_x = [sem(f"ld_x{n}") for n in range(XL)]
        consts = sem("consts")
        consts2 = sem("consts2")
        c_act, cT_ps, cT_ok, mod_ps, rows_ok, modT_ps, modT_ok, keep_ok, rows_stored = (
            sem(n) for n in ("c_act", "cT_ps", "cT_ok", "mod_ps", "rows_ok", "modT_ps", "modT_ok",
                             "keep_ok", "rows_stored"))
        dve_step = sem("dve_step")
        w_ps, w_hi, w_lo = sem("w_ps"), sem("w_hi"), sem("w_lo")
        ln1_var, ln1_sd, ln1_ok, ln1_stat = (sem(n) for n in ("ln1_var", "ln1_sd", "ln1_ok", "ln1_stat"))
        nat_ld = [sem(f"nat_ld{n}") for n in range(2)]
        pair_ps, pair_hi, pair_lo = sem("pair_ps"), sem("pair_hi"), sem("pair_lo")
        xh_ok, xhT_ps, hT_ok, proj_ps, state_ok, attn_ps = (
            sem(n) for n in ("xh_ok", "xhT_ps", "hT_ok", "proj_ps", "state_ok", "attn_ps"))
        bca_ld, bcb_ld, xb_ok, gated_ok, x2_ok, stat2_ok, var2_ok, sd2_ok, rs2_ok, nm2_ok = (
            sem(n) for n in ("bca_ld", "bcb_ld", "xb_ok", "gated_ok", "x2_ok", "stat2_ok",
                             "var2_ok", "sd2_ok", "rs2_ok", "nm2_ok"))
        xh2_ok, h2m_ok, h2_ok, h16hi_ok, h16lo_ok, h16T_ps, h16T_ok, logit_ps, logit_ok, hid_stored = (
            sem(n) for n in ("xh2_ok", "h2m_ok", "h2_ok", "h16hi_ok", "h16lo_ok", "h16T_ps",
                             "h16T_ok", "logit_ps", "logit_ok", "hid_stored"))
        gateb_ld = sem("gateb_ld")
        r_neg, r_exp, r_u, r_ln, r_sp, r_score, r_picked, rank_ps, te_ok, te_ps = (
            sem(n) for n in ("r_neg", "r_exp", "r_u", "r_ln", "r_sp", "r_score", "r_picked",
                             "rank_ps", "te_ok", "te_ps"))
        hot_ok, hot_used, slots_ok, route_ok = (
            sem(n) for n in ("hot_ok", "hot_used", "slots_ok", "route_ok"))
        col_ok = sem("col_ok")
        gathered = [sem(f"gathered{n}") for n in range(U)]
        xT_ps, xT_ok, gu_ps, clip_ok, silu_ok, hid_ok, hidT_ps, hidhi_ok, hidlo_ok, y_ps, y_ok = (
            sem(n) for n in ("xT_ps", "xT_ok", "gu_ps", "clip_ok", "silu_ok", "hid_ok", "hidT_ps",
                             "hidhi_ok", "hidlo_ok", "y_ps", "y_ok"))
        y_stored = [sem(f"y_stored{n}") for n in range(U)]
        colc_ok = sem("colc_ok")
        yg_ld = [sem(f"yg_ld{n}") for n in range(2)]
        shared_ld = [sem(f"shared_ld{n}") for n in range(2)]
        comb_step, fin_ok = sem("comb_step"), sem("fin_ok")
        out_stored = [sem(f"out_stored{n}") for n in range(2)]

        block = ctx.enter_context(nc.Block())

        PARTS = ((0, 0), (0, 1), (1, 0))

        def mixer_steps(engine, body):
            body(0, True, False)
            body(1, True, True)
            with engine.Fori(2, B) as s:
                body(s, True, True)
            body(B, False, True)

        DEPTH = 5

        def tile_steps(engine, group):
            group(0, 0, U)
            group(1, 0, U)
            with engine.Fori(2, AT // U) as i:
                group(i, 0, U)
            group(AT // U, 0, U)
            group(AT // U + 1, 0, DEPTH + 1 - U)

        def tile(i, q, behind):
            g, slot = i + (q - behind) // U, (q - behind) % U
            if isinstance(g, int) and not 0 <= g * U + slot < AT:
                return None
            return U * g + slot, slot, g

        @block.sync
        def _(sp):
            sp.dma_start(c_s[:, :], cond).then_inc(ld_cond, 16)
            for n in range(XL):
                a, b = n * NT // XL, (n + 1) * NT // XL
                sp.dma_start(xs[:, a:b, :], x_t[:, a:b, :]).then_inc(ld_x[n], 16)
            for w, src in enumerate((w_in, w_out)):
                sp.dma_start(wa_n[:, w, :, :], src.rearrange("(c p) d -> p c d", p=P)).then_inc(ld_attn, 16)
            sp.dma_start(nat_sh[:, 0, :], sh_gate).then_inc(ld_shared, 16)
            sp.dma_start(nat_sh[:, 1, :], sh_up).then_inc(ld_shared, 16)
            sp.dma_start(nat_sh[:, 2, :].rearrange("p (r i) -> p r i", i=I),
                         sh_down.rearrange("(r p) i -> p r i", p=P)).then_inc(ld_shared, 16)

            def load_pair(pair, slot):
                e = ds(2 * pair, 2)
                sp.dma_start(nat[:, slot, 0, :, :], gate_w[e, :, :].rearrange("e i d -> i e d"))\
                  .then_inc(nat_ld[slot], 16)
                sp.dma_start(nat[:, slot, 1, :, :], up_w[e, :, :].rearrange("e i d -> i e d"))\
                  .then_inc(nat_ld[slot], 16)
                for j in range(2):
                    sp.dma_start(nat[:, slot, 2, j, :].rearrange("p (r i) -> p r i", i=I),
                                 down_w[ds(2 * pair + j, 1), :, :].rearrange("e (r p) i -> p (e r) i", p=P))\
                      .then_inc(nat_ld[slot], 16)

            for h in range(2):
                load_pair(h, h)
            sp.wait_ge(rows_ok, 1)
            sp.dma_start(mod_dram, rows[:, :, :].rearrange("b r d -> b (r d)")).then_inc(rows_stored, 16)
            sp.wait_ge(rows_stored, 16)
            mod_v = mod_dram.rearrange("b (r d) -> b r d", d=D)

            def load_rows(dst, b, first, semaphore):
                sp.dma_start(dst[:, :, :], mod_v[ds(b, 1), first:first + 2, :].to_broadcast([P, 2, D]))\
                  .then_inc(semaphore, 16)

            load_rows(bc_a, 0, GA, bca_ld)
            load_rows(bc_b, 0, CB, bcb_ld)
            for b in range(B):
                sp.dma_start(gate_b[:, b:b + 1, :], mod_v[b:b + 1, GB:GB + 1, :].to_broadcast([P, 1, D]))\
                  .then_inc(gateb_ld, 16)

            def body(s, front, back):
                if back:
                    b = s - 1
                    sp.wait_ge(h16lo_ok, TPB * b + TPB)
                    sp.dma_start(hid_t[:, ds(TPB * b, TPB), :], h16[:, :, :]).then_inc(hid_stored, 16)
                    if not isinstance(s, int) or s < B:
                        sp.wait_ge(h2_ok, TPB * b + TPB)
                        load_rows(bc_b, s, CB, bcb_ld)
                if front:
                    at_least(sp, xb_ok, s + 1)
                    at_least(sp, gated_ok, TPB * s + TPB)
                    if not isinstance(s, int) or s < B - 1:
                        load_rows(bc_a, s + 1, GA, bca_ld)
                    for h in range(PPB):
                        at_least(sp, pair_ps, 3 * (PPB * s + h + 1))
                        load_pair(PPB * (s + 1) + h, h)

            body(0, True, False)
            body(1, True, True)
            with sp.Fori(2, B - 1) as s:
                body(s, True, True)
            body_last = B - 1
            sp.wait_ge(h16lo_ok, TPB * body_last)
            sp.dma_start(hid_t[:, TPB * (body_last - 1):TPB * body_last, :], h16[:, :, :]).then_inc(hid_stored, 16)
            sp.wait_ge(h2_ok, TPB * body_last)
            load_rows(bc_b, body_last, CB, bcb_ld)
            body(B, False, True)

            def store_group(dst, i, first):
                for slot in range(U):
                    sp.wait_ge(y_ok, U * i + slot + 1)
                    sp.dma_start(dst[:, ds(U * (i - first) + slot, 1), :], yo[:, slot:slot + 1, :])\
                      .then_inc(y_stored[slot], 16)

            with sp.Fori(0, RT // U) as i:
                store_group(y_t, i, 0)
            with sp.Fori(RT // U, AT // U) as i:
                store_group(shared_t, i, RT // U)
            for n in range(U):
                sp.wait_ge(y_stored[n], 16 * (AT // U))

            def comb(b):
                for u in range(TPB):
                    t = TPB * b + u
                    at_least(sp, fin_ok, t - TPB + 1)
                    sp.dma_start(yg[:, u, K:K + 1, :], shared_t[:, ds(t, 1), :]).then_inc(shared_ld[u], 16)
                for u in range(TPB):
                    if isinstance(b, int) and b == 0:
                        continue
                    t = TPB * (b - 1) + u
                    sp.dma_start(out_t[:, ds(t, 1), :], fin[:, u:u + 1, :]).then_inc(out_stored[u], 16)

            comb(0)
            with sp.Fori(1, B) as b:
                comb(b)
            for u in range(TPB):
                sp.wait_ge(fin_ok, TPB * (B - 1) + u + 1)
                sp.dma_start(out_t[:, TPB * (B - 1) + u:TPB * (B - 1) + u + 1, :], fin[:, u:u + 1, :])\
                  .then_inc(out_stored[u], 16)
            for u in range(TPB):
                sp.wait_ge(out_stored[u], 16 * B)

        @block.gpsimd
        def _(pool):
            pool.memset(ident[:, :], 0.0).then_inc(consts, 1)
            pool.iota(iota_i[:, :], pattern=[[1, P]], base=0, channel_multiplier=0).then_inc(consts, 1)
            pool.iota(part_i[:, :], pattern=[[0, 1]], base=0, channel_multiplier=1).then_inc(consts, 1)
            pool.iota(token_i[:, :], pattern=[[P, NT]], base=0, channel_multiplier=1).then_inc(consts, 1)
            pool.memset(ones16[:, :], 1.0).then_inc(consts, 1)
            pool.memset(eps_t[:, :], EPS).then_inc(consts, 1)
            pool.memset(one_t[:, :], 1.0).then_inc(consts, 1)
            pool.memset(tile_expert[:, :], E).then_inc(consts, 1)
            pool.memset(token_of[:, AT:AT + 1], 0).then_inc(consts, 1)
            pool.wait_ge(consts, 9)
            pool.affine_select(out=ident[:, :], in_=ident[:, :], compare_op=ALU.not_equal, fill=1.0,
                               base=0, pattern=[[-1, P]], channel_multiplier=1).then_inc(consts, 1)

            def body(s, front, back):
                if back:
                    b = s - 1
                    pool.wait_ge(bcb_ld, 16 * b + 16)
                    for q in range(TPB):
                        t = TPB * b + q
                        pool.wait_ge(xh2_ok, t + 1)
                        at_least(pool, h16lo_ok, TPB * b)
                        pool.tensor_tensor(h2[:, q, :], xh2[:, q, :], bc_b[:, 0, :], ALU.mult)\
                            .then_inc(h2m_ok, 1)
                        pool.wait_ge(h2m_ok, t + 1)
                        pool.tensor_tensor(h2[:, q, :], h2[:, q, :], bc_b[:, 1, :], ALU.add)\
                            .then_inc(h2_ok, 1)
                if front:
                    pool.wait_ge(xh_ok, TPB * s + TPB)
                    pool.wait_ge(bca_ld, 16 * s + 16)
                    for q in range(TPB):
                        xq = xs[:, ds(TPB * s + q, 1), :].rearrange("p a d -> p (a d)")
                        ins = pool.tensor_tensor(xq, xq, bc_a[:, 1, :], ALU.add)
                    ins.then_inc(xb_ok, 1)
                if back:
                    for q in range(TPB):
                        t = TPB * b + q
                        pool.wait_ge(h16hi_ok, t + 1)
                        pool.tensor_tensor(h16[:, q, D:HL], h2[:, q, :], h16[:, q, 0:D], ALU.subtract)\
                            .then_inc(h16lo_ok, 1)

            mixer_steps(pool, body)

            pool.wait_ge(slots_ok, 1)
            def group(i, lo, hi):
                for q in range(lo, hi):
                    if (now := tile(i, q, 0)) is None:
                        continue
                    j, slot, g = now
                    at_least(pool, xT_ps, j - U + 1)
                    pool.wait_ge(col_ok, j + 1)
                    if (after := tile(i, q, -1)) is not None:
                        at_least(pool, gathered[after[1]], 16 * after[2])
                        copy_column(j + 1, after[1])
                    pool.indirect_dma_start(xg[:, slot, :], None, hid_dram,
                                            bass.IndirectOffsetOnAxis(ap=col[:, slot:slot + 1], axis=0))\
                        .then_inc(gathered[slot], 16)

            def copy_column(j, slot):
                pool.tensor_copy(col[:, slot:slot + 1], token_of[:, ds(j, 1)]).then_inc(col_ok, 1)

            pool.wait_ge(hid_stored, 16 * B)
            copy_column(0, 0)
            tile_steps(pool, group)

            for n in range(U):
                pool.wait_ge(y_stored[n], 16 * (RT // U))

            def copy_columns(t, u):
                pool.tensor_copy(col_c[:, u, :], slot_of[:, ds(t, 1), :].rearrange("p a k -> p (a k)"))\
                    .then_inc(colc_ok, 1)

            def comb(b, last):
                for u in range(TPB):
                    t = TPB * b + u
                    at_least(pool, fin_ok, t - TPB + 1)
                    pool.wait_ge(colc_ok, t + 1)
                    if not (last and u == TPB - 1):
                        at_least(pool, yg_ld[1 - u], 16 * K * (b + u))
                        copy_columns(t + 1, 1 - u)
                    for k in range(K):
                        pool.indirect_dma_start(yg[:, u, k, :], None, y_dram,
                                                bass.IndirectOffsetOnAxis(ap=col_c[:, u, k:k + 1], axis=0))\
                            .then_inc(yg_ld[u], 16)

            copy_columns(0, 0)
            comb(0, False)
            with pool.Fori(1, B - 1) as b:
                comb(b, False)
            comb(B - 1, True)

        @block.scalar
        def _(act):
            act.dma_start(wmod_s[:, :, :], wmod.rearrange("(c p) n -> p c n", p=P)).then_inc(ld_wmod, 16)
            act.dma_start(bias8[:, :], bias.rearrange("(a d) -> a d", a=1).to_broadcast([B, D])).then_inc(ld_small, 16)
            act.dma_start(dec[:, :], decay.rearrange("(c p) -> c p", p=P)).then_inc(ld_small, 16)
            act.dma_start(rt_n[:, :], router_w).then_inc(ld_small, 16)
            act.dma_start(ebias[:, :], expert_bias.rearrange("(a e) -> a e", a=1).to_broadcast([P, E]))\
               .then_inc(ld_small, 16)
            act.wait_ge(ld_cond, 16)
            act.activation(c_s[:, :], c_s[:, :], ACT.Silu).then_inc(c_act, 1)
            act.wait_ge(ld_small, 64)
            act.activation(dec[:, :], dec[:, :], ACT.Sigmoid).then_inc(keep_ok, 1)

            act.wait_ge(w_ps, 3)
            act.activation(rt_T[:, :, 0, :], bank[4][:, 0:C * E].rearrange("p (c e) -> p c e", e=E),
                           ACT.Copy, scale=SPLIT).then_inc(w_hi, 1)
            act.activation(wgu[:, E, :, 0, :], bank[5][:, :].rearrange("p (c n) -> p c n", c=C),
                           ACT.Copy, scale=SPLIT).then_inc(w_hi, 1)
            act.activation(wdn[:, E, 0, :], bank[6][:, 0:D], ACT.Copy, scale=SPLIT).then_inc(w_hi, 1)

            act.wait_ge(ln1_var, NT)
            act.activation(sd1[:, :], mv1[:, :, 1], ACT.Sqrt, bias=eps_t[:, :]).then_inc(ln1_sd, 1)

            def pair_hi_half(pair):
                for j in range(2):
                    act.wait_ge(pair_ps, 3 * pair + j + 1)
                    act.activation(wgu[:, ds(2 * pair + j, 1), :, 0, :].rearrange("p a c n -> p (a c) n"),
                                   bank[5 + j][:, :].rearrange("p (c n) -> p c n", c=C),
                                   ACT.Copy, scale=SPLIT).then_inc(pair_hi, 1)
                act.wait_ge(pair_ps, 3 * pair + 3)
                act.activation(wdn[:, ds(2 * pair, 2), 0, :], bank[7][:, :].rearrange("p (a d) -> p a d", a=2),
                               ACT.Copy, scale=SPLIT).then_inc(pair_hi, 1)

            def body(s, front, back):
                if front:
                    act.wait_ge(xhT_ps, s + 1)
                    at_least(act, proj_ps, s)
                    if isinstance(s, int) and s == 0:
                        act.wait_ge(modT_ok, 2)
                    for c in range(C):
                        act.activation(hT[:, c, :], bank[0][:, c * S:(c + 1) * S], ACT.Identity,
                                       scale=modT[:, C + c, ds(s, 1)], bias=modT[:, c, ds(s, 1)])\
                           .then_inc(hT_ok, 1)
                    pair_hi_half(PPB * s)
                if back:
                    b = s - 1
                    at_least(act, hid_stored, 16 * b)
                    at_least(act, h16T_ps, b)
                    for q in range(TPB):
                        act.wait_ge(h2_ok, TPB * b + q + 1)
                        act.activation(h16[:, q, 0:D], h2[:, q, :], ACT.Copy).then_inc(h16hi_ok, 1)
                if front:
                    for h in range(1, PPB):
                        pair_hi_half(PPB * s + h)
                if back:
                    act.wait_ge(h16T_ps, b + 1)
                    at_least(act, logit_ps, b)
                    act.activation(h16T[:, :, :, :].rearrange("p q c t -> p (q c t)"), bank16[3], ACT.Copy)\
                       .then_inc(h16T_ok, 1)
                    act.wait_ge(logit_ps, b + 1)
                    act.activation(logits[:, ds(TPB * b, TPB), :],
                                   bank[4][:, 0:TPB * E].rearrange("p (q e) -> p q e", e=E),
                                   ACT.Copy, scale=1.0 / SPLIT).then_inc(logit_ok, 1)
                if front:
                    act.wait_ge(var2_ok, TPB * s + TPB)
                    at_least(act, rs2_ok, s)
                    act.activation(sd2[:, :], mv2[:, :, 1], ACT.Sqrt, bias=eps_t[:, :]).then_inc(sd2_ok, 1)

            mixer_steps(act, body)

            act.wait_ge(r_neg, 1)
            act.activation(r1, r0, ACT.Exp).then_inc(r_exp, 1)
            act.wait_ge(r_u, 1)
            act.activation(r3, r2, ACT.Ln).then_inc(r_ln, 1)
            act.wait_ge(r_sp, 1)
            act.activation(score, r0, ACT.Sqrt).then_inc(r_score, 1)

            def group(i, lo, hi):
                for q in range(lo, hi):
                    if (now := tile(i, q, 2)) is not None:
                        j, slot, g = now
                        act.wait_ge(clip_ok, j + 1)
                        at_least(act, hid_ok, j - U + 1)
                        act.activation(act_g[:, slot, :], clip[:, slot, 0:I], ACT.Silu, scale=1.0 / SPLIT)\
                           .then_inc(silu_ok, 1)
                    if (now := tile(i, q, 0)) is not None:
                        j, slot, g = now
                        act.wait_ge(xT_ps, j + 1)
                        at_least(act, gu_ps, j - U + 1)
                        act.activation(xT[:, slot, :, :].rearrange("p c t -> p (c t)"),
                                       bank16[slot % 2][:, 0:2 * C * P], ACT.Copy).then_inc(xT_ok, 1)
                    if (now := tile(i, q, 3)) is not None:
                        j, slot, g = now
                        act.wait_ge(hidT_ps, j + 1)
                        at_least(act, y_ps, j - U + 1)
                        act.activation(hidT[:, slot, 0, :], bank[4 + slot % 2][:, 0:P], ACT.Copy)\
                           .then_inc(hidhi_ok, 1)

            tile_steps(act, group)

        @block.vector
        def _(dve):
            steps = [0]

            def then(ins):
                steps[0] += 1
                ins.then_inc(dve_step, 1)
                dve.wait_ge(dve_step, steps[0])

            dve.wait_ge(consts, 10)
            dve.tensor_copy(part_f[:, :], part_i[:, :]).then_inc(consts2, 1)
            dve.tensor_copy(token_f[:, :], token_i[:, :]).then_inc(consts2, 1)
            dve.tensor_copy(ident16[:, :], ident[:, :]).then_inc(consts2, 1)
            dve.tensor_copy(iota16[:, :], iota_i[:, :]).then_inc(consts2, 1)
            dve.tensor_copy(iota32[:, :], iota_i[:, 0:E]).then_inc(consts2, 1)
            dve.tensor_copy(token_of[:, RT:AT], token_i[:, :]).then_inc(consts2, 1)
            dve.wait_ge(consts2, 6)
            dve.tensor_scalar(before16[:, :], iota16[:, :], part_f[:, :], None, ALU.is_gt).then_inc(consts2, 1)

            dve.wait_ge(cT_ps, 1)
            dve.tensor_copy(cT[:, :, :], bank[3][:, 0:C * B].rearrange("p (c b) -> p c b", b=B)).then_inc(cT_ok, 1)
            then(dve.tensor_copy(keep[:, :], bank[3][:, C * B:C * B + C]))
            then(dve.tensor_scalar(omk[:, :], keep[:, :], -1.0, 1.0, ALU.mult, ALU.add))
            dve.wait_ge(ld_attn, 32)
            for c in range(C):
                dve.tensor_scalar(wa_k[:, c, :], wa_n[:, 0, c, :], omk[:, c:c + 1], None, ALU.mult)\
                   .then_inc(keep_ok, 1)

            dve.wait_ge(mod_ps, 1)
            for n, (bk, half) in enumerate(((1, 0), (2, 1))):
                g = bank[bk][0:B, half * D:(half + 1) * D]
                dve.tensor_scalar(rows_a[:, n, :], g, 0.0, 2.0, ALU.is_ge, ALU.mult).then_inc(dve_step, 1)
            dve.tensor_copy(rows[:, SB, :], bank[1][0:B, D:2 * D]).then_inc(dve_step, 1)
            dve.tensor_scalar(rows[:, CB, :], bank[2][0:B, 0:D], 1.0, None, ALU.add).then_inc(dve_step, 1)
            steps[0] += 4
            dve.wait_ge(dve_step, steps[0])
            then(dve.tensor_scalar(rows_a, rows_a, -1.0, None, ALU.add))
            for n, (bk, half) in enumerate(((1, 0), (2, 1))):
                ins = dve.tensor_tensor(rows_b[:, n, :], bank[bk][0:B, half * D:(half + 1) * D], rows_a[:, n, :],
                                        ALU.mult)
            then(ins)
            for n, r in enumerate((GA, GB)):
                then(dve.scalar_tensor_tensor(rows[:, r, :], rows_b[:, n, :], GATE_MIN, rows_a[:, n, :],
                                              ALU.max, ALU.mult))
            dve.wait_ge(ld_small, 64)
            dve.tensor_tensor(rows[:, GAB, :], rows[:, GA, :], bias8[:, :], ALU.mult).then_inc(rows_ok, 1)
            dve.wait_ge(modT_ps, 1)
            dve.tensor_copy(modT[:, 0:C, :], bank[7][:, 64:64 + C * B].rearrange("p (c b) -> p c b", b=B))\
               .then_inc(modT_ok, 1)
            dve.tensor_scalar(modT[:, C:2 * C, :], bank[7][:, 64 + C * B:64 + 2 * C * B]
                              .rearrange("p (c b) -> p c b", b=B), 1.0, None, ALU.add).then_inc(modT_ok, 1)

            dve.wait_ge(w_hi, 1)
            dve.scalar_tensor_tensor(rt_T[:, :, 1, :], bank[4][:, 0:C * E].rearrange("p (c e) -> p c e", e=E),
                                     SPLIT, rt_T[:, :, 0, :], ALU.mult, ALU.subtract).then_inc(w_lo, 1)
            dve.wait_ge(w_hi, 2)
            dve.scalar_tensor_tensor(wgu[:, E, :, 1, :], bank[5][:, :].rearrange("p (c n) -> p c n", c=C),
                                     SPLIT, wgu[:, E, :, 0, :], ALU.mult, ALU.subtract).then_inc(w_lo, 1)
            dve.wait_ge(w_hi, 3)
            dve.scalar_tensor_tensor(wdn[:, E, 1, :], bank[6][:, 0:D], SPLIT, wdn[:, E, 0, :],
                                     ALU.mult, ALU.subtract).then_inc(w_lo, 1)
            dve.wait_ge(w_ps, 5)
            for w in range(2):
                dve.tensor_copy(wa_T[:, w, :, :], bank[w][:, :].rearrange("p (c e) -> p c e", c=C))\
                   .then_inc(w_lo, 1)

            for t in range(0, NT, 2):
                if t % (NT // XL) == 0:
                    dve.wait_ge(ld_x[t * XL // NT], 16)
                for q in range(2):
                    if t:
                        dve.wait_ge(ln1_var, t + q - 1)
                    dve.bn_stats(stats[:, q, :], xs[:, t + q, :]).then_inc(ln1_stat, 1)
                for q in range(2):
                    dve.wait_ge(ln1_stat, t + q + 1)
                    dve.bn_aggr(mv1[:, t + q, :], stats[:, q, :]).then_inc(ln1_var, 1)
            dve.wait_ge(ln1_sd, 1)
            then(dve.reciprocal(rs1[:, :], sd1[:, :]))
            then(dve.scalar_tensor_tensor(nm1[:, :], mv1[:, :, 0], -1.0, rs1[:, :], ALU.mult, ALU.mult))

            def pair_lo_half(pair, parts=(0, 1, 2)):
                for j in parts:
                    dve.wait_ge(pair_hi, 3 * pair + j + 1)
                    if j < 2:
                        w = wgu[:, ds(2 * pair + j, 1), :, :, :].rearrange("p a c h n -> p (a c) h n")
                    else:
                        w = wdn[:, ds(2 * pair, 2), :, :]
                    dve.scalar_tensor_tensor(w[:, :, 1, :], bank[5 + j][:, :].rearrange("p (c n) -> p c n", c=2),
                                             SPLIT, w[:, :, 0, :], ALU.mult, ALU.subtract).then_inc(pair_lo, 1)

            def body(s, front, back):
                if front:
                    at_least(dve, xhT_ps, s)
                    for q in range(TPB):
                        t = TPB * s + q
                        dve.tensor_scalar(xh[:, q, :], xs[:, ds(t, 1), :].rearrange("p a d -> p (a d)"),
                                          rs1[:, ds(t, 1)], nm1[:, ds(t, 1)], ALU.mult, ALU.add).then_inc(xh_ok, 1)
                if back:
                    b = s - 1
                    dve.wait_ge(sd2_ok, b + 1)
                    dve.reciprocal(rs2[:, :], sd2[:, :]).then_inc(rs2_ok, 1)
                    dve.wait_ge(rs2_ok, b + 1)
                    dve.scalar_tensor_tensor(nm2[:, :], mv2[:, :, 0], -1.0, rs2[:, :], ALU.mult, ALU.mult)\
                       .then_inc(nm2_ok, 1)
                    dve.wait_ge(nm2_ok, b + 1)
                    for q in range(TPB):
                        t = TPB * b + q
                        at_least(dve, h2m_ok, t - TPB + 1)
                        dve.tensor_scalar(xh2[:, q, :], xs[:, ds(t, 1), :].rearrange("p a d -> p (a d)"),
                                          rs2[:, q:q + 1], nm2[:, q:q + 1], ALU.mult, ALU.add).then_inc(xh2_ok, 1)
                if front:
                    pair_lo_half(PPB * s)
                    dve.wait_ge(proj_ps, s + 1)
                    at_least(dve, attn_ps, s)
                    for c in range(C):
                        dve.tensor_tensor_scan(st[:, c, :], keep[:, c:c + 1].to_broadcast([P, S]),
                                               bank[1][:, c * S:(c + 1) * S], 0.0, ALU.mult, ALU.add)\
                           .then_inc(state_ok, 1)
                    dve.wait_ge(attn_ps, s + 1)
                    dve.wait_ge(bca_ld, 16 * s + 16)
                    for q in range(TPB):
                        dve.tensor_tensor(gated[:, q, :], bank[2][:, q * D:(q + 1) * D], bc_a[:, 0, :], ALU.mult)\
                           .then_inc(gated_ok, 1)
                    dve.wait_ge(xb_ok, s + 1)
                    for q in range(TPB):
                        t = TPB * s + q
                        dve.wait_ge(gated_ok, t + 1)
                        xq = xs[:, ds(t, 1), :].rearrange("p a d -> p (a d)")
                        dve.tensor_tensor(xq, xq, gated[:, q, :], ALU.add).then_inc(x2_ok, 1)
                    dve.wait_ge(x2_ok, TPB * s + TPB)
                    pair_lo_half(PPB * s + 1, (0, 1))
                    for q in range(TPB):
                        t = TPB * s + q
                        dve.bn_stats(stats2[:, q, :], xs[:, ds(t, 1), :].rearrange("p a d -> p (a d)"))\
                           .then_inc(stat2_ok, 1)
                    dve.wait_ge(stat2_ok, TPB * s + TPB)
                    pair_lo_half(PPB * s + 1, (2,))
                    for q in range(TPB):
                        dve.bn_aggr(mv2[:, q, :], stats2[:, q, :]).then_inc(var2_ok, 1)

            mixer_steps(dve, body)

            lg = logits[:, :, :]
            dve.wait_ge(logit_ok, B)
            dve.scalar_tensor_tensor(r0, lg, -1.0, lg, ALU.mult, ALU.min).then_inc(r_neg, 1)
            dve.wait_ge(r_exp, 1)
            dve.tensor_scalar(r2, r1, 1.0, None, ALU.add).then_inc(r_u, 1)
            dve.wait_ge(r_u, 1)
            then(dve.tensor_scalar(r0, r2, -1.0, None, ALU.add))
            then(dve.tensor_scalar(r4, r0, 0.0, None, ALU.is_equal))
            then(dve.tensor_tensor(r0, r0, r4, ALU.add))
            then(dve.reciprocal(r0, r0))
            then(dve.tensor_tensor(r0, r0, r1, ALU.mult))
            dve.wait_ge(r_ln, 1)
            then(dve.tensor_tensor(r3, r3, r4, ALU.add))
            then(dve.tensor_tensor(r3, r3, r0, ALU.mult))
            then(dve.tensor_scalar(r4, lg, 0.0, None, ALU.max))
            dve.tensor_tensor(r0, r3, r4, ALU.add).then_inc(r_sp, 1)
            dve.wait_ge(r_score, 1)
            then(dve.tensor_tensor(r1, score, ebias[:, :].rearrange("p (a e) -> p a e", a=1)
                                   .to_broadcast([P, NT, E]), ALU.add))
            for t in range(NT):
                ins = dve.max(top_v[:, t, :], r1[:, t, :])
            then(ins)
            for t in range(NT):
                ins = dve.max_index(top_i[:, t, :], top_v[:, t, :], r1[:, t, :])
            then(ins)
            then(dve.tensor_copy(top_f[:, :, :], top_i[:, :, 0:K].rearrange("p t k -> p k t")))
            for k in range(K):
                ins = dve.tensor_tensor(
                    chosen[:, k, :, :], iota32[:, :].rearrange("p (a e) -> p a e", a=1).to_broadcast([P, NT, E]),
                    top_f[:, k, :].rearrange("p (t a) -> p t a", a=1).to_broadcast([P, NT, E]), ALU.is_equal)
            then(ins)
            dve.tensor_tensor(r2, chosen[:, 0, :, :], chosen[:, 1, :, :], ALU.add)
            then(dve.tensor_tensor(r3, chosen[:, 2, :, :], chosen[:, 3, :, :], ALU.add))
            dve.tensor_tensor(picked[:, :, :], r2, r3, ALU.add).then_inc(r_picked, 1)
            dve.wait_ge(rank_ps, 1)
            then(dve.tensor_scalar(tiles_i[:, :], bank[1][:, 0:E], float(P - 1), None, ALU.add))
            then(dve.tensor_scalar(tiles_i[:, :], tiles_i[:, :], 7, None, ALU.logical_shift_right))
            then(dve.tensor_copy(tiles_f[:, :], tiles_i[:, :]))
            then(dve.tensor_tensor_scan(last_tile[:, :], one_t[:, :].to_broadcast([P, E]), tiles_f[:, :], 0.0,
                                        ALU.mult, ALU.add))
            then(dve.tensor_tensor(first_tile[:, :], last_tile[:, :], tiles_f[:, :], ALU.subtract))
            then(dve.scalar_tensor_tensor(
                r0, first_tile[:, :].rearrange("p (a e) -> p a e", a=1).to_broadcast([P, NT, E]), float(P),
                bank[0][:, :].rearrange("p (t e) -> p t e", e=E), ALU.mult, ALU.add))
            for k in range(K):
                then(dve.tensor_tensor((r1, r2)[k % 2], chosen[:, k, :, :], r0, ALU.mult))
                ins = dve.tensor_reduce(slot_f[:, k, :], (r1, r2)[k % 2], AX.X, ALU.add)
            then(ins)
            then(dve.tensor_copy(slot_of[:, :, :], slot_f[:, :, :].rearrange("p k t -> p t k")))
            then(dve.tensor_scalar(slot_tmp[:, :, :], slot_of[:, :, :], 7, None, ALU.logical_shift_right))
            dve.tensor_copy(slot_tile[:, :, :], slot_tmp[:, :, :])
            then(dve.tensor_scalar(slot_row[:, :, :], slot_tmp[:, :, :], -float(P), None, ALU.mult))
            then(dve.tensor_tensor(slot_row[:, :, :], slot_row[:, :, :], slot_f[:, :, :].rearrange("p k t -> p t k"),
                                   ALU.add))
            then(dve.tensor_scalar(te_cmp[:, :], first_tile[:, :], part_f[:, :], None, ALU.is_le))
            then(dve.tensor_reduce(te_col[:, :], te_cmp[:, :], AX.X, ALU.add))
            dve.tensor_scalar(te_col[:, :], te_col[:, :], -1.0, None, ALU.add).then_inc(te_ok, 1)

            def hots(t):
                for k in range(K):
                    at_least(dve, hot_used, K * (t - 1) + k + 1)
                    dve.tensor_scalar(row_hot[:, k, :], iota16[:, :],
                                      slot_row[:, ds(t, 1), k:k + 1].rearrange("p a b -> p (a b)"), None,
                                      ALU.is_equal)
                    dve.tensor_scalar(tile_hot[:, k, :], iota16[:, :],
                                      slot_tile[:, ds(t, 1), k:k + 1].rearrange("p a b -> p (a b)"),
                                      token_f[:, ds(t, 1)], ALU.is_equal, ALU.mult).then_inc(hot_ok, 1)

            hots(0)
            with dve.Fori(1, NT) as t:
                hots(t)
            dve.wait_ge(te_ps, 1)
            dve.tensor_copy(tile_expert[0:1, U:U + RT], bank[3][0:1, 0:RT]).then_inc(route_ok, 1)
            dve.wait_ge(hot_used, K * NT)
            dve.tensor_copy(token_of[:, 0:RT], bank[2][:, 0:RT]).then_inc(slots_ok, 1)
            for k in range(K):
                then(dve.tensor_tensor((r1, r2)[k % 2], chosen[:, k, :, :], score, ALU.mult))
                ins = dve.tensor_reduce(prob[:, k, :], (r1, r2)[k % 2], AX.X, ALU.add)
            then(ins)
            then(dve.tensor_reduce(prob_sum[:, :], prob[:, :, :].rearrange("p k t -> p t k"), AX.X, ALU.add))
            then(dve.tensor_scalar(prob_sum[:, :], prob_sum[:, :], 1e-20, SPLIT * SPLIT, ALU.add, ALU.mult))
            then(dve.reciprocal(prob_sum[:, :], prob_sum[:, :]))
            then(dve.tensor_tensor(weight[:, :, :], prob[:, :, :].rearrange("p k t -> p t k"),
                                   prob_sum[:, :].rearrange("p (t a) -> p t a", a=1).to_broadcast([P, NT, K]),
                                   ALU.mult))

            def group(i, lo, hi):
                for q in range(lo, hi):
                    if (now := tile(i, q, 5)) is not None:
                        j, slot, g = now
                        dve.wait_ge(y_ps, j + 1)
                        at_least(dve, y_stored[slot], 16 * g)
                        dve.tensor_copy(yo[:, slot, :], bank[6 + slot % 2][:, 0:D]).then_inc(y_ok, 1)
                    if (now := tile(i, q, 2)) is not None:
                        j, slot, g = now
                        dve.wait_ge(silu_ok, j + 1)
                        at_least(dve, hidT_ps, j - U + 1)
                        dve.tensor_tensor(hid[:, slot, :], act_g[:, slot, :], clip[:, slot, I:2 * I], ALU.mult)\
                           .then_inc(hid_ok, 1)
                    if (now := tile(i, q, 1)) is not None:
                        j, slot, g = now
                        dve.wait_ge(gu_ps, j + 1)
                        at_least(dve, hid_ok, j - U + 1)
                        dve.tensor_scalar(clip[:, slot, :], bank[2 + slot % 2][:, 0:2 * I], CLAMP * SPLIT,
                                          -CLAMP * SPLIT, ALU.min, ALU.max).then_inc(clip_ok, 1)
                    if (now := tile(i, q, 3)) is not None:
                        j, slot, g = now
                        dve.wait_ge(hidhi_ok, j + 1)
                        dve.tensor_tensor(hidT[:, slot, 1, :], bank[4 + slot % 2][:, 0:P], hidT[:, slot, 0, :],
                                          ALU.subtract).then_inc(hidlo_ok, 1)

            tile_steps(dve, group)

            CS = K + 2
            dve.wait_ge(gateb_ld, 16 * B)

            def comb(b):
                for u in range(TPB):
                    t = TPB * b + u
                    dve.wait_ge(yg_ld[u], 16 * K * b + 16 * K)
                    dve.wait_ge(shared_ld[u], 16 * b + 16)
                    w = weight[:, ds(t, 1), :].rearrange("p a k -> p (a k)")
                    a = [acc[:, 2 * u + n % 2, :] for n in range(CS)]
                    dve.tensor_scalar(a[0], yg[:, u, 0, :], w[:, 0:1], None, ALU.mult).then_inc(comb_step, 1)
                    for k in range(1, K):
                        dve.wait_ge(comb_step, CS * t + k)
                        dve.scalar_tensor_tensor(a[k], yg[:, u, k, :], w[:, k:k + 1], a[k - 1],
                                                 ALU.mult, ALU.add).then_inc(comb_step, 1)
                    dve.wait_ge(comb_step, CS * t + K)
                    dve.scalar_tensor_tensor(a[K], yg[:, u, K, :], 1.0 / (SPLIT * SPLIT), a[K - 1],
                                             ALU.mult, ALU.add).then_inc(comb_step, 1)
                    dve.wait_ge(comb_step, CS * t + K + 1)
                    dve.tensor_tensor(a[K + 1], a[K], gate_b[:, ds(b, 1), :].rearrange("p a d -> p (a d)"),
                                      ALU.mult).then_inc(comb_step, 1)
                    dve.wait_ge(comb_step, CS * t + K + 2)
                    at_least(dve, out_stored[u], 16 * b)
                    dve.tensor_tensor(fin[:, u, :], a[K + 1], xs[:, ds(t, 1), :].rearrange("p a d -> p (a d)"),
                                      ALU.add).then_inc(fin_ok, 1)

            comb(0)
            with dve.Fori(1, B) as b:
                comb(b)

        @block.tensor
        def _(pe):
            pe.wait_ge(consts, 10)
            pe.wait_ge(c_act, 1)
            for c in range(C):
                ins = pe.transpose(bank[3][:, c * B:(c + 1) * B], c_s[:, c * P:(c + 1) * P], ident[0:B, 0:B])
            pe.wait_ge(keep_ok, 1)
            pe.transpose(bank[3][:, C * B:C * B + C], dec[:, :], ident[0:C, 0:C]).then_inc(cT_ps, 1)
            pe.wait_ge(cT_ok, 1)
            pe.wait_ge(ld_wmod, 16)
            for n in range(3):
                for c in range(C):
                    ins = pe.matmul(bank[n][0:B, :], cT[:, c, :], wmod_s[:, c, n * 512:(n + 1) * 512],
                                    start=(c == 0), stop=(c == C - 1))
            ins.then_inc(mod_ps, 1)
            for n in range(2 * C):
                for c in range(C):
                    ins = pe.matmul(bank[7][:, 64 + n * B:64 + (n + 1) * B], wmod_s[:, c, n * P:(n + 1) * P],
                                    cT[:, c, :], start=(c == 0), stop=(c == C - 1))
            ins.then_inc(modT_ps, 1)
            pe.wait_ge(ld_small, 64)
            for c in range(C):
                ins = pe.transpose(bank[4][:, c * E:(c + 1) * E], rt_n[:, c * P:(c + 1) * P], ident[0:E, 0:E])
            ins.then_inc(w_ps, 1)
            pe.wait_ge(ld_shared, 48)
            for c in range(C):
                for m in range(2):
                    ins = pe.transpose(bank[5][:, (2 * c + m) * P:(2 * c + m + 1) * P],
                                       nat_sh[:, m, c * P:(c + 1) * P], ident[:, :])
            ins.then_inc(w_ps, 1)
            for r in range(C):
                ins = pe.transpose(bank[6][:, r * P:(r + 1) * P], nat_sh[:, 2, r * I:(r + 1) * I], ident[:, :])
            ins.then_inc(w_ps, 1)
            pe.wait_ge(rows_ok, 1)
            pe.wait_ge(keep_ok, 1 + C)
            for w, src in enumerate((wa_k[:, :, :], wa_n[:, 1, :, :])):
                for c in range(C):
                    for e in range(C):
                        ins = pe.transpose(bank[w][:, c * D + e * P:c * D + (e + 1) * P],
                                           src[:, e, c * P:(c + 1) * P], ident[:, :])
                ins.then_inc(w_ps, 1)
            pe.wait_ge(w_lo, 5)
            pe.wait_ge(modT_ok, 2)

            def pair_T(pair, slot):
                pe.wait_ge(nat_ld[slot], 64 * (pair // PPB) + 64 if isinstance(pair, int) else pair)

            def body(s, front, back):
                def transposes(h):
                    pair = PPB * s + h
                    pe.wait_ge(nat_ld[h], 64 * s + 64)
                    for j in range(2):
                        at_least(pe, pair_lo, 3 * (pair - 1) + j + 1)
                        for c in range(C):
                            for m in range(2):
                                ins = pe.transpose(bank[5 + j][:, (2 * c + m) * P:(2 * c + m + 1) * P],
                                                   nat[:, h, m, j, c * P:(c + 1) * P], ident[:, :])
                        ins.then_inc(pair_ps, 1)
                    at_least(pe, pair_lo, 3 * pair)
                    for j in range(2):
                        for r in range(C):
                            ins = pe.transpose(bank[7][:, j * D + r * P:j * D + (r + 1) * P],
                                               nat[:, h, 2, j, r * I:(r + 1) * I], ident[:, :])
                    ins.then_inc(pair_ps, 1)

                if front:
                    pe.wait_ge(xh_ok, TPB * s + TPB)
                    at_least(pe, hT_ok, C * s)
                    for q in range(TPB):
                        for c in range(C):
                            ins = pe.transpose(bank[0][:, c * S + q * P:c * S + (q + 1) * P],
                                               xh[:, q, c * P:(c + 1) * P], ident[:, :])
                    ins.then_inc(xhT_ps, 1)
                    transposes(0)
                    pe.wait_ge(hT_ok, C * s + C)
                    at_least(pe, state_ok, C * s)
                    for e in range(C):
                        for c in range(C):
                            ins = pe.matmul(bank[1][:, e * S:(e + 1) * S], wa_T[:, 0, c, e * P:(e + 1) * P],
                                            hT[:, c, :], start=(c == 0), stop=(c == C - 1))
                    ins.then_inc(proj_ps, 1)
                    for h in range(1, PPB):
                        transposes(h)
                if back:
                    b = s - 1
                    pe.wait_ge(h16lo_ok, TPB * b + TPB)
                    at_least(pe, h16T_ok, b)
                    for q in range(TPB):
                        for n in range(2 * C):
                            ins = pe.transpose(bank16[3][:, (q * 2 * C + n) * P:(q * 2 * C + n + 1) * P],
                                               h16[:, q, n * P:(n + 1) * P], ident16[:, :])
                    ins.then_inc(h16T_ps, 1)
                if front:
                    pe.wait_ge(state_ok, C * s + C)
                    at_least(pe, gated_ok, TPB * s)
                    for q in range(TPB):
                        for c in range(C):
                            ins = pe.matmul(bank[2][:, q * D:(q + 1) * D], st[:, c, q * P:(q + 1) * P],
                                            wa_T[:, 1, c, :], start=(c == 0), stop=(c == C - 1))
                    ins.then_inc(attn_ps, 1)
                if back:
                    pe.wait_ge(h16T_ok, b + 1)
                    at_least(pe, logit_ok, b)
                    for q in range(TPB):
                        for n, (c, (a, m)) in enumerate((c, p) for c in range(C) for p in PARTS):
                            ins = pe.matmul(bank[4][:, q * E:(q + 1) * E], h16T[:, q, a * C + c, :],
                                            rt_T[:, c, m, :], start=(n == 0), stop=(n == 3 * C - 1))
                    ins.then_inc(logit_ps, 1)

            mixer_steps(pe, body)

            pe.wait_ge(r_picked, 1)
            flat = picked[:, :, :].rearrange("p t e -> p (t e)")
            pe.matmul(bank[0][:, :], before16[:, :], flat, start=True, stop=False)
            for t in range(NT - 1):
                n = NT - 1 - t
                pe.matmul(bank[0][:, (t + 1) * E:].rearrange("p (t e) -> p t e", e=E), ones16[:, :],
                          picked[:, t:t + 1, :].to_broadcast([P, n, E]), start=False, stop=(n == 1))
            for t in range(NT):
                ins = pe.matmul(bank[1][:, 0:E], ones16[:, :], picked[:, t, :], start=(t == 0), stop=(t == NT - 1))
            ins.then_inc(rank_ps, 1)
            pe.wait_ge(te_ok, 1)
            pe.matmul(bank[3][0:1, 0:P], te_col[:, :], ident[:, :], start=True, stop=True).then_inc(te_ps, 1)

            def slots(t, first, last):
                for k in range(K):
                    pe.wait_ge(hot_ok, K * t + k + 1)
                    pe.matmul(bank[2][:, 0:P], row_hot[:, k, :], tile_hot[:, k, :],
                              start=(first and k == 0), stop=(last and k == K - 1)).then_inc(hot_used, 1)

            slots(0, True, False)
            with pe.Fori(1, NT - 1) as t:
                slots(t, False, False)
            slots(NT - 1, False, True)
            pe.wait_ge(slots_ok, 1)
            pe.wait_ge(route_ok, 1)

            regs = [pe.alloc_register(f"tile_expert{n}") for n in range(2 * U)]

            def group(i, lo, hi):
                pe.load(regs, tile_expert[0:1, ds(U * i, 2 * U)])
                expert = [pe.snap(r, min_val=0, max_val=E) for r in regs]
                for q in range(lo, hi):
                    if (now := tile(i, q, 0)) is not None:
                        j, slot, g = now
                        pe.wait_ge(gathered[slot], 16 * g + 16)
                        at_least(pe, xT_ok, j - 1)
                        for n in range(2 * C):
                            ins = pe.transpose(bank16[slot % 2][:, n * P:(n + 1) * P],
                                               xg[:, slot, n * P:(n + 1) * P], ident16[:, :])
                        ins.then_inc(xT_ps, 1)
                    if (now := tile(i, q, 1)) is not None:
                        j, slot, g = now
                        pe.wait_ge(xT_ok, j + 1)
                        at_least(pe, clip_ok, j - 1)
                        w = wgu[:, ds(expert[U + q - 1], 1), :, :, :].rearrange("p a c h n -> p (a c) h n")
                        for n, (c, (a, m)) in enumerate((c, p) for c in range(C) for p in PARTS):
                            ins = pe.matmul(bank[2 + slot % 2][:, 0:2 * I], xT[:, slot, a * C + c, :],
                                            w[:, c, m, :], start=(n == 0), stop=(n == 3 * C - 1))
                        ins.then_inc(gu_ps, 1)
                    if (now := tile(i, q, 3)) is not None:
                        j, slot, g = now
                        pe.wait_ge(hid_ok, j + 1)
                        at_least(pe, hidlo_ok, j - 1)
                        pe.transpose(bank[4 + slot % 2][:, 0:P], hid[:, slot, :], ident[:, :]).then_inc(hidT_ps, 1)
                    if (now := tile(i, q, 4)) is not None:
                        j, slot, g = now
                        pe.wait_ge(hidlo_ok, j + 1)
                        at_least(pe, y_ok, j - 1)
                        w = wdn[:, ds(expert[U + q - 4], 1), :, :].rearrange("p a h d -> p (a h) d")
                        for n, (a, m) in enumerate(PARTS):
                            ins = pe.matmul(bank[6 + slot % 2][:, 0:D], hidT[:, slot, a, :], w[:, m, :],
                                            start=(n == 0), stop=(n == 2))
                        ins.then_inc(y_ps, 1)

            tile_steps(pe, group)


_INS = ["L0_attn_x", "L0_attn_W_in", "L0_attn_W_out", "L0_attn_decay", "L0_attn_bias",
        "L0_ffn_router_w", "L0_ffn_expert_bias", "L0_ffn_gate_w", "L0_ffn_up_w", "L0_ffn_down_w",
        "L0_ffn_shared_gate_w", "L0_ffn_shared_up_w", "L0_ffn_shared_down_w", "L0_c", "L0_wmod"]


def kernel(**inputs):
    import numpy as _np
    import concourse.bacc as _bacc
    from concourse import mybir as _mybir
    from concourse.bass_utils import run_bass_kernel_spmd as _run

    nc = _bacc.Bacc("TRN2", target_bir_lowering=False, num_devices=1)
    arrays, args = {}, []
    for name in _INS:
        a = _np.ascontiguousarray(inputs[name])
        arrays[f"in_{name}_dram"] = a
        args.append(nc.dram_tensor(f"in_{name}_dram", a.shape, _mybir.dt.from_np(a.dtype), kind="ExternalInput").ap())
    o = nc.dram_tensor("out_0_dram", inputs["L0_attn_x"].shape, _mybir.dt.float32, kind="ExternalOutput").ap()
    adaln_block(nc, *args, o)
    r = _run(nc, [arrays], core_ids=[0])
    return r.results[0]["out_0_dram"]
```

```python
from contextlib import ExitStack

import concourse.bass as bass
from concourse import mybir

fp32 = mybir.dt.float32
fp16 = mybir.dt.float16
i32 = mybir.dt.int32
u32 = mybir.dt.uint32
ALU = mybir.AluOpType
ACT = mybir.ActivationFunctionType
AX = mybir.AxisListType
ds = bass.ds

P = 128
SPLIT = 256.0
CLAMP = 7.0
EPS = 1e-5
GATE_MIN = 0.25


def at_least(engine, semaphore, value):
    if isinstance(value, int) and value <= 0:
        return
    engine.wait_ge(semaphore, value)


def adaln_block(nc, x, w_in, w_out, decay, bias, router_w, expert_bias, gate_w, up_w, down_w,
                sh_gate, sh_up, sh_down, cond, wmod, out):
    B, S, D = x.shape
    E, I, _ = gate_w.shape
    K = 4
    T = B * S
    NT = T // P
    TPB = S // P
    C = D // P
    G = 2
    U = 8
    STEPS = U // G
    RT = -(-((T * K + E * (P - 1)) // P) // U) * U
    AT = RT + NT
    NM = 6
    GA, GAB, CB, SB, GB = range(5)
    NR = 5
    PAIRS = E // 2
    PPB = PAIRS // B
    HL = 2 * D
    DEPTH = 4
    CS = K + 1
    HT = 2
    CU = 4

    x_t = x.rearrange("b s d -> (b s) d").rearrange("(t p) d -> p t d", p=P)
    out_t = out.rearrange("b s d -> (b s) d").rearrange("(t p) d -> p t d", p=P)
    mod_dram = nc.dram_tensor("mod_rows_dram", (B, NR * D), fp32, kind="Internal").ap()
    hid_dram = nc.dram_tensor("hidden_dram", (T, HL), fp16, kind="Internal").ap()
    y_dram = nc.dram_tensor("expert_out_dram", (RT * P, D), fp32, kind="Internal").ap()
    hid_t = hid_dram.rearrange("(t p) d -> p t d", p=P)
    y_t = y_dram.rearrange("(t p) d -> p t d", p=P)

    ctx = ExitStack()
    with ctx:
        def sb(name, shape, dt):
            return ctx.enter_context(nc.sbuf_tensor(name, shape, dt))

        def sem(name):
            return ctx.enter_context(nc.semaphore(name))

        xs = sb("xs", [P, NT, D], fp32)
        wgu = sb("wgu", [P, E + 1, C, 2, 2 * I], fp16)
        wdn = sb("wdn", [P, E + 1, 2, D], fp16)
        ident = sb("ident", [P, P], fp32)
        ident16 = sb("ident16", [P, P], fp16)
        iota_i = sb("iota_i", [P, P], i32)
        iota16 = sb("iota16", [P, P], fp16)
        iota32 = sb("iota32", [P, E], fp32)
        part_i = sb("part_i", [P, 1], i32)
        part_f = sb("part_f", [P, 1], fp32)
        token_i = sb("token_i", [P, NT], i32)
        token_f = sb("token_f", [P, NT], fp32)
        before16 = sb("before16", [P, P], fp16)
        ones16 = sb("ones16", [P, P], fp16)
        eps_t = sb("eps_t", [P, 1], fp32)
        one_t = sb("one_t", [P, 1], fp32)
        ebias = sb("ebias", [P, E], fp32)
        logits = sb("logits", [P, NT, E], fp32)
        gate_b = sb("gate_b", [P, B, D], fp32)
        slot_of = sb("slot_of", [P, NT, K], i32)
        token_of = sb("token_of", [P, AT + 1], i32)
        weight = sb("weight", [P, NT, K], fp32)
        tile_expert = sb("tile_expert", [1, G * DEPTH + AT + 2 * U], i32)
        wmod_s = sb("wmod_s", [P, C, NM * D], fp32)
        c_s = sb("c_s", [B, D], fp32)
        cT = sb("cT", [P, C, B], fp32)
        bias8 = sb("bias8", [B, D], fp32)
        rows = sb("rows", [B, NR, D], fp32)
        rows_a = sb("rows_a", [B, 2, D], fp32)
        rows_b = sb("rows_b", [B, 2, D], fp32)
        modT = sb("modT", [P, 2 * C, B], fp32)
        dec = sb("dec", [C, P], fp32)
        keep = sb("keep", [P, C], fp32)
        omk = sb("omk", [P, C], fp32)
        wa_n = sb("wa_n", [P, 2, C, D], fp32)
        wa_k = sb("wa_k", [P, C, D], fp32)
        wa_T = sb("wa_T", [P, 2, C, D], fp32)
        rt_n = sb("rt_n", [E, D], fp32)
        rt_T = sb("rt_T", [P, C, 2, E], fp16)
        nat = sb("nat", [P, 2, 3, 2, D], fp32)
        nat_sh = sb("nat_sh", [P, 3, D], fp32)
        stats = sb("stats", [P, 2, 6], fp32)
        mv1 = sb("mv1", [P, NT, 2], fp32)
        sd1 = sb("sd1", [P, NT], fp32)
        rs1 = sb("rs1", [P, NT], fp32)
        nm1 = sb("nm1", [P, NT], fp32)
        bc = sb("bc", [P, 2, 2, D], fp32)
        bc_a, bc_b = bc[:, 0, :, :], bc[:, 1, :, :]
        mix_room = sb("mix_room", [P, 6, 2 * D], fp32)
        xh, gated, xh2, h2 = (mix_room[:, n, :].rearrange("p (q d) -> p q d", q=TPB) for n in range(4))
        hT, st = (mix_room[:, n, :].rearrange("p (c t) -> p c t", c=C) for n in (4, 5))
        stats2 = sb("stats2", [P, TPB, 6], fp32)
        mv2 = sb("mv2", [P, TPB, 2], fp32)
        sd2 = sb("sd2", [P, TPB], fp32)
        rs2 = sb("rs2", [P, TPB], fp32)
        nm2 = sb("nm2", [P, TPB], fp32)
        h16 = sb("h16", [P, TPB, HL], fp16)
        h16T = sb("h16T", [P, TPB, 2 * C, P], fp16)

        room = wmod_s[:, :, :].rearrange("p c n -> p (c n)")

        def routing_room(n):
            return room[:, n * NT * E:(n + 1) * NT * E].rearrange("p (t e) -> p t e", e=E)
        r0, r1, r2, r3, r4, score = (routing_room(n) for n in range(6))
        top_v = sb("top_v", [P, NT, 8], fp32)
        top_i = sb("top_i", [P, NT, 8], u32)
        top16 = sb("top16", [P, NT, K], fp16)
        chosen = sb("chosen", [P, NT, E, K], fp16)
        pairs16 = r3.bitcast(fp16).rearrange("p t (e k) -> p t e k", k=K // 2)
        picked = sb("picked", [P, NT, E], fp16)
        tiles_i = sb("tiles_i", [P, E], i32)
        tiles_f = sb("tiles_f", [P, E], fp32)
        last_tile = sb("last_tile", [P, E], fp32)
        first_tile = sb("first_tile", [P, E], fp32)
        slot_f = sb("slot_f", [P, NT, K], fp32)
        slot_tmp = sb("slot_tmp", [P, NT, K], i32)
        slot_tile = sb("slot_tile", [P, NT, K], fp16)
        slot_row = sb("slot_row", [P, NT, K], fp16)
        prob = sb("prob", [P, K, NT], fp32)
        prob_sum = sb("prob_sum", [P, NT], fp32)
        te_cmp = sb("te_cmp", [P, E], fp32)
        te_col = sb("te_col", [P, 1], fp32)
        HK = HT * K

        def hot_room(room16, columns):
            return room16.rearrange("p (c m) -> p c m", m=HK)[:, 0:columns, :]
        iota_rep = hot_room(mix_room[:, 0, :].bitcast(fp16), P)
        row_hot = [hot_room(mix_room[:, 1 + n, :].bitcast(fp16), P) for n in range(2)]
        tile_hot = [hot_room(mix_room[:, 3 + n, :].bitcast(fp16), RT) for n in range(2)]
        tile_token = [hot_room(r.bitcast(fp16), RT)
                      for r in (mix_room[:, 5, :], nat_sh[:, :, :].rearrange("p a d -> p (a d)"))]
        col = sb("col", [P, STEPS, G], i32)
        nat_rows = nat[:, :, :, :, :].rearrange("p a b c d -> p (a b c) d")
        xg = nat_rows[:, 0:U, :].rearrange("p u n -> p (u n)").bitcast(fp16)\
            .rearrange("p (u g n) -> p u g n", u=STEPS, g=G)
        hidT = room[:, 0:NT * E].bitcast(fp16).rearrange("p (u a g n) -> p u a g n", u=2, a=2, g=G)
        xT = bc[:, :, :, :].rearrange("p a b d -> p (a b d)").bitcast(fp16)\
            .rearrange("p (u g c t) -> p u g c t", u=2, g=G, c=2 * C)
        clip = mix_room[:, 0:2, :].rearrange("p u (g n) -> p u g n", g=G)
        yo = mix_room[:, 2:4, :].rearrange("p u (g n) -> p u g n", g=G)
        act_g = mix_room[:, 4, :].rearrange("p (u g n) -> p u g n", u=2, g=G)
        hid = mix_room[:, 5, :].rearrange("p (u g n) -> p u g n", u=2, g=G)
        yg = wgu[:, 0:CU * K * D * 4 // (C * 2 * 2 * I * 2), :, :, :].rearrange("p e c h n -> p (e c h n)")\
            .bitcast(fp32).rearrange("p (u k d) -> p u k d", u=CU, k=K)
        col_c = slot_tmp[:, 0:CU, :]
        acc = nat_rows[:, 0:2 * CU, :]
        fin = nat_rows[:, 2 * CU:3 * CU, :]

        bank = [ctx.enter_context(nc.psum_tensor(f"bank{n}", [P, 512], fp32)) for n in range(8)]
        bank16 = [b[:, :].bitcast(fp16) for b in bank]

        ld_cond, ld_decay, ld_wmod, ld_small, ld_attn, ld_shared = (
            sem(n) for n in ("ld_cond", "ld_decay", "ld_wmod", "ld_small", "ld_attn", "ld_shared"))
        XL = 4
        ld_x = [sem(f"ld_x{n}") for n in range(XL)]
        consts = sem("consts")
        consts2 = sem("consts2")
        c_act, cT_ps, cT_ok, mod_ps, rows_ok, modT_ps, modT_ok, keep_ok, rows_stored = (
            sem(n) for n in ("c_act", "cT_ps", "cT_ok", "mod_ps", "rows_ok", "modT_ps", "modT_ok",
                             "keep_ok", "rows_stored"))
        dve_step = sem("dve_step")
        w_ps, wa_ok, w_hi, w_lo = (sem(n) for n in ("w_ps", "wa_ok", "w_hi", "w_lo"))
        dec_ps, gates_step = sem("dec_ps"), sem("gates_step")
        ln1_var, ln1_sd, ln1_ok, ln1_stat = (sem(n) for n in ("ln1_var", "ln1_sd", "ln1_ok", "ln1_stat"))
        nat_ld = [sem(f"nat_ld{n}") for n in range(2)]
        pair_ps, pair_hi, pair_lo = sem("pair_ps"), sem("pair_hi"), sem("pair_lo")
        xh_ok, xhT_ps, hT_ok, proj_ps, state_ok, attn_ps = (
            sem(n) for n in ("xh_ok", "xhT_ps", "hT_ok", "proj_ps", "state_ok", "attn_ps"))
        bcg_ld, bca_ld, bcb_ld, xb_ok, gated_ok, x2_ok, stat2_ok, var2_ok, sd2_ok, rs2_ok, nm2_ok = (
            sem(n) for n in ("bcg_ld", "bca_ld", "bcb_ld", "xb_ok", "gated_ok", "x2_ok", "stat2_ok",
                             "var2_ok", "sd2_ok", "rs2_ok", "nm2_ok"))
        xh2_ok, h2m_ok, h2_ok, h16hi_ok, h16lo_ok, h16T_ps, h16T_ok, logit_ps, logit_ok, hid_stored = (
            sem(n) for n in ("xh2_ok", "h2m_ok", "h2_ok", "h16hi_ok", "h16lo_ok", "h16T_ps",
                             "h16T_ok", "logit_ps", "logit_ok", "hid_stored"))
        gateb_ld = sem("gateb_ld")
        r_neg, r_exp, r_u, r_ln, r_sp, r_score, r_picked, count_ps, rank_ps, te_ok, te_ps = (
            sem(n) for n in ("r_neg", "r_exp", "r_u", "r_ln", "r_sp", "r_score", "r_picked",
                             "count_ps", "rank_ps", "te_ok", "te_ps"))
        iota_ok, row_ok, tile_ok, token_ok = (sem(n) for n in ("iota_ok", "row_ok", "tile_ok", "token_ok"))
        hot_used, slots_ok, route_ok = (
            sem(n) for n in ("hot_used", "slots_ok", "route_ok"))
        col_ok = sem("col_ok")
        gathered = [sem(f"gathered{n}") for n in range(STEPS)]
        xT_ps, xT_ok, gu_ps, clip_ok, silu_ok, hid_ok, hidT_ps, hidhi_ok, hidlo_ok, y_ps, y_ok = (
            sem(n) for n in ("xT_ps", "xT_ok", "gu_ps", "clip_ok", "silu_ok", "hid_ok", "hidT_ps",
                             "hidhi_ok", "hidlo_ok", "y_ps", "y_ok"))
        y_stored = [sem(f"y_stored{n}") for n in range(2)]
        colc_ok = sem("colc_ok")
        yg_ld = [sem(f"yg_ld{n}") for n in range(CU)]
        sh_rows = [sem(f"sh_rows{n}") for n in range(STEPS)]
        shy_ok, shx_ok = sem("shy_ok"), sem("shx_ok")
        comb_step, fin_ok = sem("comb_step"), sem("fin_ok")
        out_stored = [sem(f"out_stored{n}") for n in range(CU)]

        block = ctx.enter_context(nc.Block())

        PARTS = ((0, 0), (0, 1), (1, 0))

        UNITS = 3 * PPB

        def mixer_steps(engine, body):
            for s in range(3):
                body(s)
            with engine.Fori(3, B - 1) as s:
                body(s)
            for s in range(B - 1, B + 3):
                body(s)

        def batch(b):
            return not isinstance(b, int) or 0 <= b < B

        def last_batch(b):
            return isinstance(b, int) and b == B - 1

        def pair_weights(s, u):
            first, j = 2 * (PPB * s + u // 3), u % 3
            if j < 2:
                return wgu[:, ds(first + j, 1), :, :, :].rearrange("p a c h n -> p (a c) h n"), j
            return wdn[:, ds(first, 2), :, :], j

        def rows_of(b):
            return xs[:, ds(TPB * b, TPB), :]

        def hot_steps(step):
            for h in range(NT // HT):
                step(h, h % 2, h == 0, h == NT // HT - 1)


        def pair_steps(engine, group):
            group(0)
            group(1)
            with engine.Fori(2, RT // U) as i:
                group(i)
            for i in range(RT // U, AT // U + 1):
                group(i)

        def pair(i, q, lag):
            body, place = i + (q - lag) // STEPS, (q - lag) % STEPS
            if isinstance(body, int) and not 0 <= body < AT // U:
                return None
            return STEPS * body + place, place % 2, place, body

        def shared(i, j):
            return isinstance(i, int) and j >= RT // G

        @block.sync
        def _(sp):
            sp.dma_start(c_s[:, :], cond).then_inc(ld_cond, 16)

            def load_x(n):
                a, b = n * NT // XL, (n + 1) * NT // XL
                sp.dma_start(xs[:, a:b, :], x_t[:, a:b, :]).then_inc(ld_x[n], 16)

            load_x(0)
            for w, src in enumerate((w_in, w_out)):
                sp.dma_start(wa_n[:, w, :, :], src.rearrange("(c p) d -> p c d", p=P)).then_inc(ld_attn, 16)
            for n in range(1, XL):
                load_x(n)
            sp.dma_start(nat_sh[:, 0, :], sh_gate).then_inc(ld_shared, 16)
            sp.dma_start(nat_sh[:, 1, :], sh_up).then_inc(ld_shared, 16)
            sp.dma_start(nat_sh[:, 2, :].rearrange("p (r i) -> p r i", i=I),
                         sh_down.rearrange("(r p) i -> p r i", p=P)).then_inc(ld_shared, 16)

            def load_pair(pair, slot):
                e = ds(2 * pair, 2)
                sp.dma_start(nat[:, slot, 0, :, :], gate_w[e, :, :].rearrange("e i d -> i e d"))\
                  .then_inc(nat_ld[slot], 16)
                sp.dma_start(nat[:, slot, 1, :, :], up_w[e, :, :].rearrange("e i d -> i e d"))\
                  .then_inc(nat_ld[slot], 16)
                for j in range(2):
                    sp.dma_start(nat[:, slot, 2, j, :].rearrange("p (r i) -> p r i", i=I),
                                 down_w[ds(2 * pair + j, 1), :, :].rearrange("e (r p) i -> p (e r) i", p=P))\
                      .then_inc(nat_ld[slot], 16)

            for h in range(2):
                load_pair(h, h)
            def next_first_pair(s):
                sp.wait_ge(pair_ps, UNITS * s + 3)
                load_pair(PPB * (s + 1), 0)

            sp.wait_ge(rows_ok, 1)
            sp.dma_start(mod_dram, rows[:, :, :].rearrange("b r d -> b (r d)")).then_inc(rows_stored, 16)
            next_first_pair(0)
            sp.wait_ge(rows_stored, 16)
            mod_v = mod_dram.rearrange("b (r d) -> b r d", d=D)

            def load_rows(dst, b, first, semaphore):
                sp.dma_start(dst[:, :, :], mod_v[ds(b, 1), first:first + 2, :].to_broadcast([P, 2, D]))\
                  .then_inc(semaphore, 16)

            def load_row(n, b, row, semaphore):
                sp.dma_start(bc_a[:, n:n + 1, :], mod_v[ds(b, 1), row:row + 1, :].to_broadcast([P, 1, D]))\
                  .then_inc(semaphore, 16)

            load_row(1, 0, GAB, bca_ld)
            load_row(0, 0, GA, bcg_ld)
            load_rows(bc_b, 0, CB, bcb_ld)

            def body(s):
                if batch(s) and batch(s + 1):
                    if not (isinstance(s, int) and s == 0):
                        next_first_pair(s)
                    sp.wait_ge(xb_ok, s + 1)
                    load_row(1, s + 1, GAB, bca_ld)
                if batch(s) and batch(s - 1):
                    sp.wait_ge(gated_ok, s)
                    load_row(0, s, GA, bcg_ld)
                if batch(s - 2) and batch(s - 1):
                    sp.wait_ge(h2_ok, s - 1)
                    load_rows(bc_b, s - 1, CB, bcb_ld)
                if batch(s) and batch(s + 1):
                    for h in range(1, PPB):
                        sp.wait_ge(pair_ps, UNITS * s + 3 * h + 3)
                        load_pair(PPB * (s + 1) + h, h)
                if batch(s - 2):
                    sp.wait_ge(h16lo_ok, s - 1)
                    sp.dma_start(hid_t[:, ds(TPB * (s - 2), TPB), :], h16[:, :, :]).then_inc(hid_stored, 16)

            mixer_steps(sp, body)
            for b in range(B):
                sp.dma_start(gate_b[:, b:b + 1, :], mod_v[b:b + 1, GB:GB + 1, :].to_broadcast([P, 1, D]))\
                  .then_inc(gateb_ld, 16)

            def store_y(j, slot):
                sp.wait_ge(y_ok, j + 1)
                sp.dma_start(y_t[:, ds(G * j, G), :], yo[:, slot, :, :]).then_inc(y_stored[slot], 16)

            def load_shared(j):
                sp.wait_ge(xT_ps, j - STEPS + 1)
                t = G * j - RT
                sp.dma_start(xg[:, j % STEPS, :, :], hid_t[:, t:t + G, :]).then_inc(sh_rows[j % STEPS], 16)

            RPAIRS, APAIRS = RT // G, AT // G
            AHEAD = STEPS + DEPTH + 1
            looped = (RPAIRS - AHEAD) // 2
            sp.wait_ge(hid_stored, 16 * B)
            with sp.Fori(0, looped) as i:
                for slot in range(2):
                    store_y(2 * i + slot, slot)
            for j in range(2 * looped, RPAIRS):
                store_y(j, j % 2)
                if RPAIRS <= j + AHEAD < APAIRS:
                    load_shared(j + AHEAD)
            for slot in range(2):
                sp.wait_ge(y_stored[slot], 16 * (RPAIRS // 2))

            def comb(i):
                for u in range(CU):
                    sp.wait_ge(fin_ok, CU * i + u + 1)
                    sp.dma_start(out_t[:, ds(CU * i + u, 1), :], fin[:, u:u + 1, :])\
                      .then_inc(out_stored[u], 16)

            with sp.Fori(0, NT // CU) as i:
                comb(i)
            for u in range(CU):
                sp.wait_ge(out_stored[u], 16 * (NT // CU))

        @block.gpsimd
        def _(pool):
            pool.memset(ident[:, :], 0.0).then_inc(consts, 1)
            pool.iota(iota_i[:, :], pattern=[[1, P]], base=0, channel_multiplier=0).then_inc(consts, 1)
            pool.iota(part_i[:, :], pattern=[[0, 1]], base=0, channel_multiplier=1).then_inc(consts, 1)
            pool.iota(token_i[:, :], pattern=[[P, NT]], base=0, channel_multiplier=1).then_inc(consts, 1)
            pool.memset(ones16[:, :], 1.0).then_inc(consts, 1)
            pool.memset(eps_t[:, :], EPS).then_inc(consts, 1)
            pool.memset(one_t[:, :], 1.0).then_inc(consts, 1)
            pool.memset(tile_expert[:, :], E).then_inc(consts, 1)
            pool.memset(token_of[:, AT:AT + 1], 0).then_inc(consts, 1)
            pool.wait_ge(consts, 9)
            pool.affine_select(out=ident[:, :], in_=ident[:, :], compare_op=ALU.not_equal, fill=1.0,
                               base=0, pattern=[[-1, P]], channel_multiplier=1).then_inc(consts, 1)

            def body(s):
                if batch(s):
                    pool.wait_ge(xh_ok, s + 1)
                    pool.wait_ge(bca_ld, 16 * s + 16)
                    pool.tensor_tensor(rows_of(s), rows_of(s), bc_a[:, 1:2, :].to_broadcast([P, TPB, D]), ALU.add)\
                        .then_inc(xb_ok, 1)
                b = s - 2
                if batch(b) and not last_batch(b):
                    pool.wait_ge(xh2_ok, b + 1)
                    pool.wait_ge(bcb_ld, 16 * b + 16)
                    at_least(pool, h16lo_ok, b)
                    pool.tensor_tensor(h2, xh2, bc_b[:, 0:1, :].to_broadcast([P, TPB, D]), ALU.mult)\
                        .then_inc(h2m_ok, 1)
                    pool.wait_ge(h2m_ok, b + 1)
                    pool.tensor_tensor(h2, h2, bc_b[:, 1:2, :].to_broadcast([P, TPB, D]), ALU.add)\
                        .then_inc(h2_ok, 1)
                    pool.wait_ge(h16hi_ok, b + 1)
                    pool.tensor_tensor(h16[:, :, D:HL], h2, h16[:, :, 0:D], ALU.subtract).then_inc(h16lo_ok, 1)

            mixer_steps(pool, body)

            pool.wait_ge(consts2, 4)
            pool.wait_ge(logit_ps, B)
            pool.tensor_copy(iota_rep, iota16[:, :].rearrange("p (c m) -> p c m", m=1).to_broadcast([P, P, HK]))\
                .then_inc(iota_ok, 1)

            pool.wait_ge(slots_ok, 1)
            pool.wait_ge(hid_stored, 16 * B)

            def copy_column(j, place):
                pool.tensor_copy(col[:, place, :], token_of[:, ds(G * j, G)]).then_inc(col_ok, 1)

            def group(i):
                for q in range(STEPS):
                    now = pair(i, q, 0)
                    if now is None or shared(i, now[0]):
                        continue
                    j, slot, place, body = now
                    at_least(pool, xT_ps, j - STEPS + 1)
                    pool.wait_ge(col_ok, j + 1)
                    j_next, _, place_next, body_next = pair(i, q, -1)
                    at_least(pool, gathered[place_next], 16 * G * body_next)
                    copy_column(j_next, place_next)
                    for g in range(G):
                        pool.indirect_dma_start(xg[:, place, g, :], None, hid_dram,
                                                bass.IndirectOffsetOnAxis(ap=col[:, place, g:g + 1], axis=0))\
                            .then_inc(gathered[place], 16)

            copy_column(0, 0)
            pair_steps(pool, group)

            for slot in range(2):
                pool.wait_ge(y_stored[slot], 16 * (RT // G // 2))

            def copy_columns(t, u):
                pool.tensor_copy(col_c[:, u, :], slot_of[:, ds(t, 1), :].rearrange("p a k -> p (a k)"))\
                    .then_inc(colc_ok, 1)

            def comb(i, last=False):
                for u in range(CU):
                    t = CU * i + u
                    at_least(pool, comb_step, CS * (t - CU) + K)
                    pool.wait_ge(colc_ok, t + 1)
                    if not (last and u == CU - 1):
                        v = (u + 1) % CU
                        at_least(pool, yg_ld[v], 16 * K * (i + (u + 1) // CU))
                        copy_columns(t + 1, v)
                    for k in range(K):
                        pool.indirect_dma_start(yg[:, u, k, :], None, y_dram,
                                                bass.IndirectOffsetOnAxis(ap=col_c[:, u, k:k + 1], axis=0))\
                            .then_inc(yg_ld[u], 16)

            copy_columns(0, 0)
            comb(0)
            with pool.Fori(1, NT // CU - 1) as i:
                comb(i)
            comb(NT // CU - 1, True)

        @block.scalar
        def _(act):
            act.dma_start(dec[:, :], decay.rearrange("(c p) -> c p", p=P)).then_inc(ld_decay, 16)
            act.dma_start(wmod_s[:, :, :], wmod.rearrange("(c p) n -> p c n", p=P)).then_inc(ld_wmod, 16)
            act.dma_start(bias8[:, :], bias.rearrange("(a d) -> a d", a=1).to_broadcast([B, D])).then_inc(ld_small, 16)
            act.dma_start(rt_n[:, :], router_w).then_inc(ld_small, 16)
            act.dma_start(ebias[:, :], expert_bias.rearrange("(a e) -> a e", a=1).to_broadcast([P, E]))\
               .then_inc(ld_small, 16)
            act.wait_ge(ld_cond, 16)
            act.activation(c_s[:, :], c_s[:, :], ACT.Silu).then_inc(c_act, 1)
            act.wait_ge(ld_decay, 16)
            act.activation(dec[:, :], dec[:, :], ACT.Sigmoid).then_inc(keep_ok, 1)

            for w in range(2):
                act.wait_ge(w_ps, w + 1)
                act.activation(wa_T[:, w, :, :], bank[(7, 4)[w]][:, :].rearrange("p (c e) -> p c e", c=C), ACT.Copy)\
                   .then_inc(wa_ok, 1)

            act.wait_ge(ln1_var, NT)
            act.activation(sd1[:, :], mv1[:, :, 1], ACT.Sqrt, bias=eps_t[:, :]).then_inc(ln1_sd, 1)

            act.wait_ge(w_ps, 3)
            act.activation(rt_T[:, :, 0, :], bank[6][:, D:D + C * E].rearrange("p (c e) -> p c e", e=E),
                           ACT.Copy, scale=SPLIT).then_inc(w_hi, 1)
            act.activation(wdn[:, E, 0, :], bank[6][:, 0:D], ACT.Copy, scale=SPLIT).then_inc(w_hi, 1)
            act.wait_ge(w_ps, 4)
            act.activation(wgu[:, E, :, 0, :], bank[5][:, :].rearrange("p (c n) -> p c n", c=C),
                           ACT.Copy, scale=SPLIT).then_inc(w_hi, 1)

            def hi_half(s, u):
                act.wait_ge(pair_ps, UNITS * s + u + 1)
                w, j = pair_weights(s, u)
                act.activation(w[:, :, 0, :], bank[5 + j][:, :].rearrange("p (c n) -> p c n", c=2),
                               ACT.Copy, scale=SPLIT).then_inc(pair_hi, 1)

            def body(s):
                if batch(s):
                    act.wait_ge(xhT_ps, s + 1)
                    if isinstance(s, int) and s == 0:
                        act.wait_ge(modT_ok, 2)
                    for c in range(C):
                        ins = act.activation(hT[:, c, :], bank[0][:, c * S:(c + 1) * S], ACT.Identity,
                                             scale=modT[:, C + c, ds(s, 1)], bias=modT[:, c, ds(s, 1)])
                    ins.then_inc(hT_ok, 1)
                    hi_half(s, 0)
                if batch(s - 2) and not last_batch(s - 2):
                    act.wait_ge(nm2_ok, s - 1)
                    for q in range(TPB):
                        ins = act.activation(xh2[:, q, :], xs[:, ds(TPB * (s - 2) + q, 1), :]
                                             .rearrange("p a d -> p (a d)"), ACT.Identity,
                                             scale=rs2[:, q:q + 1], bias=nm2[:, q:q + 1])
                    ins.then_inc(xh2_ok, 1)
                if batch(s):
                    hi_half(s, 1)
                if batch(s - 3):
                    act.wait_ge(h16T_ps, s - 2)
                    act.activation(h16T[:, :, :, :].rearrange("p q c t -> p (q c t)"), bank16[3], ACT.Copy)\
                       .then_inc(h16T_ok, 1)
                if batch(s):
                    hi_half(s, 2)
                if batch(s - 2):
                    at_least(act, hid_stored, 16 * (s - 2))
                    act.wait_ge(h2_ok, s - 1)
                    act.activation(h16[:, :, 0:D], h2, ACT.Copy).then_inc(h16hi_ok, 1)
                if last_batch(s - 2):
                    act.activation(sd2[:, 0:1], eps_t[:, :], ACT.Exp)
                if batch(s):
                    for u in range(3, UNITS - 1):
                        hi_half(s, u)
                if batch(s - 1):
                    act.wait_ge(var2_ok, s)
                    act.activation(sd2[:, :], mv2[:, :, 1], ACT.Sqrt, bias=eps_t[:, :]).then_inc(sd2_ok, 1)
                if batch(s - 3):
                    act.wait_ge(logit_ps, s - 2)
                    act.activation(logits[:, ds(TPB * (s - 3), TPB), :],
                                   bank[4][:, 0:TPB * E].rearrange("p (q e) -> p q e", e=E),
                                   ACT.Copy, scale=1.0 / SPLIT).then_inc(logit_ok, 1)
                if batch(s):
                    hi_half(s, UNITS - 1)

            mixer_steps(act, body)

            act.wait_ge(r_neg, 1)
            act.activation(r1, r0, ACT.Exp).then_inc(r_exp, 1)
            act.wait_ge(r_u, 1)
            act.activation(r3, r2, ACT.Ln).then_inc(r_ln, 1)
            act.wait_ge(r_sp, 1)
            act.activation(score, r4, ACT.Sqrt).then_inc(r_score, 1)

            def token_step(h, slot, first, last):
                act.wait_ge(tile_ok, h + 1)
                at_least(act, hot_used, h - 1)
                for u in range(HT):
                    m = slice(u * K, (u + 1) * K)
                    ins = act.activation(tile_token[slot][:, :, m], tile_hot[slot][:, :, m], ACT.Copy,
                                         scale=token_f[:, ds(HT * h + u, 1)])
                ins.then_inc(token_ok, 1)

            hot_steps(token_step)

            def group(i):
                for q in range(STEPS):
                    if (now := pair(i, q, 3)) is not None:
                        j, slot, place, body = now
                        act.wait_ge(hidT_ps, j + 1)
                        act.activation(hidT[:, slot, 0, :, :].rearrange("p g n -> p (g n)"),
                                       bank[4 + slot][:, 0:G * P], ACT.Copy).then_inc(hidhi_ok, 1)
                    if (now := pair(i, q, 0)) is not None:
                        j, slot, place, body = now
                        act.wait_ge(xT_ps, j + 1)
                        act.activation(xT[:, slot, :, :, :].rearrange("p g c t -> p (g c t)"),
                                       bank16[slot], ACT.Copy).then_inc(xT_ok, 1)
                    if (now := pair(i, q, 1)) is not None:
                        j, slot, place, body = now
                        act.wait_ge(clip_ok, j + 1)
                        act.activation(act_g[:, slot, :, :], clip[:, slot, :, 0:I], ACT.Silu, scale=1.0 / SPLIT)\
                           .then_inc(silu_ok, 1)

            pair_steps(act, group)

        @block.vector
        def _(dve):
            steps = [0]

            def then(ins):
                steps[0] += 1
                ins.then_inc(dve_step, 1)
                dve.wait_ge(dve_step, steps[0])

            dve.wait_ge(consts, 10)
            dve.tensor_copy(part_f[:, :], part_i[:, :]).then_inc(consts2, 1)
            dve.tensor_copy(token_f[:, :], token_i[:, :]).then_inc(consts2, 1)
            dve.tensor_copy(ident16[:, :], ident[:, :]).then_inc(consts2, 1)
            dve.tensor_copy(iota16[:, :], iota_i[:, :]).then_inc(consts2, 1)
            dve.tensor_copy(iota32[:, :], iota_i[:, 0:E]).then_inc(consts2, 1)
            dve.tensor_copy(token_of[:, RT:AT], token_i[:, :]).then_inc(consts2, 1)
            dve.wait_ge(consts2, 6)
            dve.tensor_scalar(before16[:, :], iota16[:, :], part_f[:, :], None, ALU.is_gt).then_inc(consts2, 1)

            dve.wait_ge(cT_ps, 1)
            dve.tensor_copy(cT[:, :, :], bank[0][:, 0:C * B].rearrange("p (c b) -> p c b", b=B)).then_inc(cT_ok, 1)
            dve.wait_ge(dec_ps, 1)
            then(dve.tensor_copy(keep[:, :], bank[3][:, 0:C]))
            then(dve.tensor_scalar(omk[:, :], keep[:, :], -1.0, 1.0, ALU.mult, ALU.add))

            def ln1_statistics(t):
                for q in range(2):
                    if t:
                        dve.wait_ge(ln1_var, t + q - 1)
                    dve.bn_stats(stats[:, q, :], xs[:, t + q, :]).then_inc(ln1_stat, 1)
                for q in range(2):
                    dve.wait_ge(ln1_stat, t + q + 1)
                    dve.bn_aggr(mv1[:, t + q, :], stats[:, q, :]).then_inc(ln1_var, 1)

            for n in range(XL):
                dve.wait_ge(ld_x[n], 16)
                for t in range(n * NT // XL, (n + 1) * NT // XL, 2):
                    ln1_statistics(t)
                if n == 0:
                    dve.wait_ge(ld_attn, 32)
                    for c in range(C):
                        dve.tensor_scalar(wa_k[:, c, :], wa_n[:, 0, c, :], omk[:, c:c + 1], None, ALU.mult)\
                           .then_inc(keep_ok, 1)
            dve.wait_ge(modT_ps, 1)
            dve.tensor_copy(modT[:, 0:C, :], bank[3][:, 64:64 + C * B].rearrange("p (c b) -> p c b", b=B))\
               .then_inc(modT_ok, 1)
            dve.tensor_scalar(modT[:, C:2 * C, :], bank[3][:, 64 + C * B:64 + 2 * C * B]
                              .rearrange("p (c b) -> p c b", b=B), 1.0, None, ALU.add).then_inc(modT_ok, 1)
            dve.wait_ge(mod_ps, 1)
            for n, (bk, half) in enumerate(((1, 0), (2, 1))):
                g = bank[bk][0:B, half * D:(half + 1) * D]
                dve.tensor_scalar(rows_a[:, n, :], g, 0.0, 2.0, ALU.is_ge, ALU.mult).then_inc(gates_step, 1)
            dve.tensor_copy(rows[:, SB, :], bank[1][0:B, D:2 * D])
            dve.tensor_scalar(rows[:, CB, :], bank[2][0:B, 0:D], 1.0, None, ALU.add)
            dve.wait_ge(ln1_sd, 1)
            then(dve.reciprocal(rs1[:, :], sd1[:, :]))
            then(dve.scalar_tensor_tensor(nm1[:, :], mv1[:, :, 0], -1.0, rs1[:, :], ALU.mult, ALU.mult))

            def normalise(b):
                for q in range(TPB):
                    t = TPB * b + q
                    ins = dve.tensor_scalar(xh[:, q, :], xs[:, ds(t, 1), :].rearrange("p a d -> p (a d)"),
                                            rs1[:, ds(t, 1)], nm1[:, ds(t, 1)], ALU.mult, ALU.add)
                ins.then_inc(xh_ok, 1)

            normalise(0)

            dve.wait_ge(w_hi, 2)
            dve.scalar_tensor_tensor(rt_T[:, :, 1, :], bank[6][:, D:D + C * E].rearrange("p (c e) -> p c e", e=E),
                                     SPLIT, rt_T[:, :, 0, :], ALU.mult, ALU.subtract).then_inc(w_lo, 1)
            dve.scalar_tensor_tensor(wdn[:, E, 1, :], bank[6][:, 0:D], SPLIT, wdn[:, E, 0, :],
                                     ALU.mult, ALU.subtract).then_inc(w_lo, 1)
            dve.wait_ge(w_hi, 3)
            dve.scalar_tensor_tensor(wgu[:, E, :, 1, :], bank[5][:, :].rearrange("p (c n) -> p c n", c=C),
                                     SPLIT, wgu[:, E, :, 0, :], ALU.mult, ALU.subtract).then_inc(w_lo, 1)

            dve.wait_ge(gates_step, 2)
            then(dve.tensor_scalar(rows_a[:, :, :], rows_a[:, :, :], -1.0, None, ALU.add))
            for n, (bk, half) in enumerate(((1, 0), (2, 1))):
                ins = dve.tensor_tensor(rows_b[:, n, :], bank[bk][0:B, half * D:(half + 1) * D], rows_a[:, n, :],
                                        ALU.mult)
            then(ins)
            for n, r in enumerate((GA, GB)):
                ins = dve.scalar_tensor_tensor(rows[:, r, :], rows_b[:, n, :], GATE_MIN, rows_a[:, n, :],
                                               ALU.max, ALU.mult)
            then(ins)
            dve.wait_ge(ld_small, 48)
            dve.tensor_tensor(rows[:, GAB, :], rows[:, GA, :], bias8[:, :], ALU.mult).then_inc(rows_ok, 1)

            def lo_half(s, u):
                dve.wait_ge(pair_hi, UNITS * s + u + 1)
                w, j = pair_weights(s, u)
                dve.scalar_tensor_tensor(w[:, :, 1, :], bank[5 + j][:, :].rearrange("p (c n) -> p c n", c=2),
                                         SPLIT, w[:, :, 0, :], ALU.mult, ALU.subtract).then_inc(pair_lo, 1)

            def body(s):
                if batch(s - 2):
                    dve.wait_ge(sd2_ok, s - 1)
                    dve.reciprocal(rs2[:, :], sd2[:, :]).then_inc(rs2_ok, 1)
                    dve.wait_ge(rs2_ok, s - 1)
                    dve.scalar_tensor_tensor(nm2[:, :], mv2[:, :, 0], -1.0, rs2[:, :], ALU.mult, ALU.mult)\
                       .then_inc(nm2_ok, 1)
                if last_batch(s - 2):
                    b = B - 1
                    dve.wait_ge(nm2_ok, b + 1)
                    dve.wait_ge(h2m_ok, b)
                    for q in range(TPB):
                        ins = dve.tensor_scalar(xh2[:, q, :], xs[:, TPB * b + q, :], rs2[:, q:q + 1],
                                                nm2[:, q:q + 1], ALU.mult, ALU.add)
                    ins.then_inc(xh2_ok, 1)
                    dve.wait_ge(xh2_ok, b + 1)
                    dve.wait_ge(bcb_ld, 16 * b + 16)
                    dve.wait_ge(h16lo_ok, b)
                    dve.tensor_tensor(h2, xh2, bc_b[:, 0:1, :].to_broadcast([P, TPB, D]), ALU.mult)\
                       .then_inc(h2m_ok, 1)
                    dve.wait_ge(h2m_ok, b + 1)
                    dve.tensor_tensor(h2, h2, bc_b[:, 1:2, :].to_broadcast([P, TPB, D]), ALU.add)\
                       .then_inc(h2_ok, 1)
                    dve.wait_ge(h16hi_ok, b + 1)
                    dve.tensor_tensor(h16[:, :, D:HL], h2, h16[:, :, 0:D], ALU.subtract).then_inc(h16lo_ok, 1)
                if batch(s) and batch(s + 1):
                    dve.wait_ge(xhT_ps, s + 1)
                    normalise(s + 1)
                if batch(s - 1):
                    lo_half(s - 1, UNITS - 1)
                if batch(s):
                    lo_half(s, 0)
                if batch(s - 1):
                    dve.wait_ge(attn_ps, s)
                    dve.wait_ge(bcg_ld, 16 * s)
                    dve.tensor_tensor(gated, bank[2][:, :].rearrange("p (q d) -> p q d", q=TPB),
                                      bc_a[:, 0:1, :].to_broadcast([P, TPB, D]), ALU.mult).then_inc(gated_ok, 1)
                if batch(s):
                    lo_half(s, 1)
                if batch(s - 1):
                    dve.wait_ge(xb_ok, s)
                    dve.wait_ge(gated_ok, s)
                    dve.tensor_tensor(rows_of(s - 1), rows_of(s - 1), gated, ALU.add).then_inc(x2_ok, 1)
                    dve.wait_ge(x2_ok, s)
                if batch(s):
                    lo_half(s, 2)
                if batch(s - 1):
                    for q in range(TPB):
                        ins = dve.bn_stats(stats2[:, q, :], xs[:, ds(TPB * (s - 1) + q, 1), :]
                                           .rearrange("p a d -> p (a d)"))
                    ins.then_inc(stat2_ok, 1)
                    dve.wait_ge(stat2_ok, s)
                if batch(s):
                    dve.wait_ge(proj_ps, s + 1)
                    for c in range(C):
                        ins = dve.tensor_tensor_scan(st[:, c, :], keep[:, c:c + 1].to_broadcast([P, S]),
                                                     bank[1][:, c * S:(c + 1) * S], 0.0, ALU.mult, ALU.add)
                    ins.then_inc(state_ok, 1)
                if batch(s - 1):
                    for q in range(TPB):
                        ins = dve.bn_aggr(mv2[:, q, :], stats2[:, q, :])
                    ins.then_inc(var2_ok, 1)
                if batch(s):
                    for u in range(3, UNITS - 1):
                        lo_half(s, u)

            mixer_steps(dve, body)

            lg = logits[:, :, :]
            dve.wait_ge(logit_ok, B)
            dve.scalar_tensor_tensor(r0, lg, -1.0, lg, ALU.mult, ALU.min).then_inc(r_neg, 1)
            dve.wait_ge(r_exp, 1)
            dve.tensor_scalar(r2, r1, 1.0, None, ALU.add).then_inc(r_u, 1)
            dve.wait_ge(r_u, 1)
            then(dve.scalar_tensor_tensor(r4, r2, -1.0, r1, ALU.add, ALU.subtract))
            then(dve.scalar_tensor_tensor(r0, lg, 0.0, r4, ALU.max, ALU.subtract))
            dve.wait_ge(r_ln, 1)
            dve.tensor_tensor(r4, r3, r0, ALU.add).then_inc(r_sp, 1)
            dve.wait_ge(r_score, 1)
            then(dve.tensor_tensor(r2, score, ebias[:, :].rearrange("p (a e) -> p a e", a=1)
                                   .to_broadcast([P, NT, E]), ALU.add))
            for t in range(NT):
                ins = dve.max(top_v[:, t, :], r2[:, t, :])
            then(ins)
            for t in range(NT):
                ins = dve.max_index(top_i[:, t, :], top_v[:, t, :], r2[:, t, :])
            then(ins)
            then(dve.tensor_copy(top16[:, :, :], top_i[:, :, 0:K]))
            dve.wait_ge(iota_ok, 1)
            then(dve.tensor_tensor(
                chosen[:, :, :, :], iota_rep[:, 0:E, 0:K].rearrange("p (a e) k -> p a e k", a=1)
                .to_broadcast([P, NT, E, K]),
                top16[:, :, :].rearrange("p t (a k) -> p t a k", a=1).to_broadcast([P, NT, E, K]), ALU.is_equal))
            then(dve.tensor_tensor(pairs16[:, :, :, :], chosen[:, :, :, 0:K // 2], chosen[:, :, :, K // 2:K],
                                   ALU.add))
            dve.tensor_tensor(picked[:, :, :], pairs16[:, :, :, 0], pairs16[:, :, :, 1], ALU.add)\
               .then_inc(r_picked, 1)
            dve.wait_ge(count_ps, 1)
            then(dve.tensor_scalar(tiles_i[:, :], bank[1][:, 0:E], float(P - 1), None, ALU.add))
            then(dve.tensor_scalar(tiles_i[:, :], tiles_i[:, :], 7, None, ALU.logical_shift_right))
            then(dve.tensor_copy(tiles_f[:, :], tiles_i[:, :]))
            then(dve.tensor_tensor_scan(last_tile[:, :], one_t[:, :].to_broadcast([P, E]), tiles_f[:, :], 0.0,
                                        ALU.mult, ALU.add))
            then(dve.tensor_tensor(first_tile[:, :], last_tile[:, :], tiles_f[:, :], ALU.subtract))
            dve.wait_ge(rank_ps, 1)
            then(dve.scalar_tensor_tensor(
                r0, first_tile[:, :].rearrange("p (a e) -> p a e", a=1).to_broadcast([P, NT, E]), float(P),
                bank[0][:, :].rearrange("p (t e) -> p t e", e=E), ALU.mult, ALU.add))
            then(dve.scalar_tensor_tensor(r1, r0, 1.0, picked[:, :, :], ALU.add, ALU.mult))
            for t in range(NT):
                ins = dve.max(top_v[:, t, :], r1[:, t, :])
            then(ins)
            dve.tensor_scalar(slot_f[:, :, :], top_v[:, :, 0:K], -1.0, None, ALU.add)
            then(dve.tensor_scalar(slot_of[:, :, :], top_v[:, :, 0:K], -1.0, None, ALU.add))
            then(dve.tensor_scalar(slot_tmp[:, :, :], slot_of[:, :, :], 7, None, ALU.logical_shift_right))
            dve.tensor_copy(slot_tile[:, :, :], slot_tmp[:, :, :])
            then(dve.scalar_tensor_tensor(slot_row[:, :, :], slot_tmp[:, :, :], -float(P), slot_f[:, :, :],
                                          ALU.mult, ALU.add))

            def hots(h, slot, first, last):
                def equal(hot, of, columns):
                    v = of[:, ds(HT * h, HT), :].rearrange("p (a t) k -> p a (t k)", a=1)
                    return dve.tensor_tensor(hot[slot], iota_rep[:, 0:columns, :],
                                             v.to_broadcast([P, columns, HK]), ALU.is_equal)

                at_least(dve, token_ok, h - 1)
                equal(tile_hot, slot_tile, RT).then_inc(tile_ok, 1)
                at_least(dve, hot_used, h - 1)
                equal(row_hot, slot_row, P).then_inc(row_ok, 1)

            hot_steps(hots)
            then(dve.tensor_scalar(te_cmp[:, :], first_tile[:, :], part_f[:, :], None, ALU.is_le))
            then(dve.tensor_reduce(te_col[:, :], te_cmp[:, :], AX.X, ALU.add))
            dve.tensor_scalar(te_col[:, :], te_col[:, :], -1.0, None, ALU.add).then_inc(te_ok, 1)
            dve.wait_ge(hot_used, NT // HT)
            dve.tensor_copy(token_of[:, 0:RT], bank[2][:, 0:RT]).then_inc(slots_ok, 1)
            dve.wait_ge(te_ps, 1)
            dve.tensor_copy(tile_expert[0:1, G * DEPTH:G * DEPTH + RT], bank[3][0:1, 0:RT]).then_inc(route_ok, 1)

            for k in range(K):
                then(dve.tensor_tensor(r2, r1, top_v[:, :, k:k + 1].to_broadcast([P, NT, E]), ALU.is_equal))
                then(dve.tensor_tensor(r3, r2, score, ALU.mult))
                ins = dve.tensor_reduce(prob[:, k, :], r3, AX.X, ALU.add)
            then(ins)
            then(dve.tensor_reduce(prob_sum[:, :], prob[:, :, :].rearrange("p k t -> p t k"), AX.X, ALU.add))
            then(dve.tensor_scalar(prob_sum[:, :], prob_sum[:, :], 1e-20, SPLIT * SPLIT, ALU.add, ALU.mult))
            then(dve.reciprocal(prob_sum[:, :], prob_sum[:, :]))
            then(dve.tensor_tensor(weight[:, :, :], prob[:, :, :].rearrange("p k t -> p t k"),
                                   prob_sum[:, :].rearrange("p (t a) -> p t a", a=1).to_broadcast([P, NT, K]),
                                   ALU.mult))

            dve.wait_ge(gateb_ld, 16 * B)

            def group(i):
                for q in range(STEPS):
                    if (now := pair(i, q, 2)) is not None:
                        j, slot, place, body = now
                        dve.wait_ge(silu_ok, j + 1)
                        dve.tensor_tensor(hid[:, slot, :, :], act_g[:, slot, :, :], clip[:, slot, :, I:2 * I],
                                          ALU.mult).then_inc(hid_ok, 1)
                    if (now := pair(i, q, 4)) is not None:
                        j, slot, place, body = now
                        products = bank[6 + slot][:, 0:G * D].rearrange("p (g n) -> p g n", g=G)
                        dve.wait_ge(y_ps, j + 1)
                        if not shared(i, j):
                            at_least(dve, y_stored[slot], 16 * (STEPS // 2 * body + place // 2))
                            dve.tensor_copy(yo[:, slot, :, :], products).then_inc(y_ok, 1)
                        else:
                            b = j - RT // G
                            if b < 2:
                                dve.wait_ge(y_stored[slot], 16 * (j // 2))
                            else:
                                dve.wait_ge(shx_ok, b - 1)
                            dve.scalar_tensor_tensor(yo[:, slot, :, :], products, 1.0 / (SPLIT * SPLIT),
                                                     gate_b[:, b:b + 1, :].to_broadcast([P, G, D]),
                                                     ALU.mult, ALU.mult).then_inc(shy_ok, 1)
                    if (now := pair(i, q, 3)) is not None:
                        j, slot, place, body = now
                        dve.wait_ge(hidhi_ok, j + 1)
                        dve.tensor_tensor(hidT[:, slot, 1, :, :].rearrange("p g n -> p (g n)"),
                                          bank[4 + slot][:, 0:G * P],
                                          hidT[:, slot, 0, :, :].rearrange("p g n -> p (g n)"),
                                          ALU.subtract).then_inc(hidlo_ok, 1)
                    if (now := pair(i, q, 1)) is not None:
                        j, slot, place, body = now
                        dve.wait_ge(gu_ps, j + 1)
                        dve.tensor_scalar(clip[:, slot, :, :].rearrange("p g n -> p (g n)"), bank[2 + slot][:, :],
                                          CLAMP * SPLIT, -CLAMP * SPLIT, ALU.min, ALU.max).then_inc(clip_ok, 1)
                    now = pair(i, q, 4)
                    if now is not None and shared(i, now[0]):
                        j, slot, place, body = now
                        b = j - RT // G
                        dve.wait_ge(shy_ok, b + 1)
                        dve.tensor_tensor(xs[:, G * b:G * b + G, :], xs[:, G * b:G * b + G, :], yo[:, slot, :, :],
                                          ALU.add).then_inc(shx_ok, 1)

            pair_steps(dve, group)

            dve.wait_ge(shx_ok, NT // G)

            def comb(i):
                for u in range(CU):
                    t = CU * i + u
                    steps_t = CS * CU * i + CS * u
                    w = weight[:, ds(t, 1), :].rearrange("p a k -> p (a k)")
                    gate = gate_b[:, ds(CU // TPB * i + u // TPB, 1), :].rearrange("p a d -> p (a d)")
                    a = [acc[:, 2 * u + n % 2, :] for n in range(CS)]
                    dve.wait_ge(yg_ld[u], 16 * K * i + 16 * K)
                    dve.tensor_scalar(a[0], yg[:, u, 0, :], w[:, 0:1], None, ALU.mult).then_inc(comb_step, 1)
                    for k in range(1, K):
                        dve.wait_ge(comb_step, steps_t + k)
                        dve.scalar_tensor_tensor(a[k], yg[:, u, k, :], w[:, k:k + 1], a[k - 1],
                                                 ALU.mult, ALU.add).then_inc(comb_step, 1)
                    dve.wait_ge(comb_step, steps_t + K)
                    dve.tensor_tensor(a[K], a[K - 1], gate, ALU.mult).then_inc(comb_step, 1)
                    dve.wait_ge(comb_step, steps_t + K + 1)
                    at_least(dve, out_stored[u], 16 * i)
                    dve.tensor_tensor(fin[:, u, :], a[K], xs[:, ds(t, 1), :].rearrange("p a d -> p (a d)"),
                                      ALU.add).then_inc(fin_ok, 1)

            comb(0)
            with dve.Fori(1, NT // CU) as i:
                comb(i)

        @block.tensor
        def _(pe):
            pe.wait_ge(consts, 10)
            pe.wait_ge(c_act, 1)
            for c in range(C):
                ins = pe.transpose(bank[0][:, c * B:(c + 1) * B], c_s[:, c * P:(c + 1) * P], ident[0:B, 0:B])
            ins.then_inc(cT_ps, 1)
            pe.wait_ge(keep_ok, 1)
            pe.transpose(bank[3][:, 0:C], dec[:, :], ident[0:C, 0:C]).then_inc(dec_ps, 1)
            pe.wait_ge(cT_ok, 1)
            pe.wait_ge(ld_wmod, 16)
            for n in (1, 2):
                for c in range(C):
                    ins = pe.matmul(bank[n][0:B, :], cT[:, c, :], wmod_s[:, c, n * 512:(n + 1) * 512],
                                    start=(c == 0), stop=(c == C - 1))
            ins.then_inc(mod_ps, 1)
            pe.wait_ge(keep_ok, 1 + C)
            for n in range(2 * C):
                for c in range(C):
                    ins = pe.matmul(bank[3][:, 64 + n * B:64 + (n + 1) * B], wmod_s[:, c, n * P:(n + 1) * P],
                                    cT[:, c, :], start=(c == 0), stop=(c == C - 1))
            ins.then_inc(modT_ps, 1)
            for w, src in enumerate((wa_k[:, :, :], wa_n[:, 1, :, :])):
                for c in range(C):
                    for e in range(C):
                        ins = pe.transpose(bank[(7, 4)[w]][:, c * D + e * P:c * D + (e + 1) * P],
                                           src[:, e, c * P:(c + 1) * P], ident[:, :])
                ins.then_inc(w_ps, 1)
            pe.wait_ge(ld_small, 48)
            for c in range(C):
                pe.transpose(bank[6][:, D + c * E:D + (c + 1) * E], rt_n[:, c * P:(c + 1) * P], ident[0:E, 0:E])
            pe.wait_ge(ld_shared, 48)
            for r in range(C):
                ins = pe.transpose(bank[6][:, r * P:(r + 1) * P], nat_sh[:, 2, r * I:(r + 1) * I], ident[:, :])
            ins.then_inc(w_ps, 1)
            for c in range(C):
                for m in range(2):
                    ins = pe.transpose(bank[5][:, (2 * c + m) * P:(2 * c + m + 1) * P],
                                       nat_sh[:, m, c * P:(c + 1) * P], ident[:, :])
            ins.then_inc(w_ps, 1)
            pe.wait_ge(wa_ok, 2)

            def transposes(s, units):
                for u in units:
                    h, j = u // 3, u % 3
                    pe.wait_ge(nat_ld[h], 64 * s + 64)
                    if isinstance(s, int) and s == 0 and u == 0:
                        pe.wait_ge(w_lo, 3)
                    at_least(pe, pair_lo, UNITS * s + u - 2)
                    if j < 2:
                        for c in range(C):
                            for m in range(2):
                                ins = pe.transpose(bank[5 + j][:, (2 * c + m) * P:(2 * c + m + 1) * P],
                                                   nat[:, h, m, j, c * P:(c + 1) * P], ident[:, :])
                    else:
                        for e in range(2):
                            for r in range(C):
                                ins = pe.transpose(bank[7][:, e * D + r * P:e * D + (r + 1) * P],
                                                   nat[:, h, 2, e, r * I:(r + 1) * I], ident[:, :])
                    ins.then_inc(pair_ps, 1)

            def body(s):
                if batch(s):
                    pe.wait_ge(xh_ok, s + 1)
                    for q in range(TPB):
                        for c in range(C):
                            ins = pe.transpose(bank[0][:, c * S + q * P:c * S + (q + 1) * P],
                                               xh[:, q, c * P:(c + 1) * P], ident[:, :])
                    ins.then_inc(xhT_ps, 1)
                if batch(s - 3):
                    pe.wait_ge(h16lo_ok, s - 2)
                    for q in range(TPB):
                        for n in range(2 * C):
                            ins = pe.transpose(bank16[3][:, (q * 2 * C + n) * P:(q * 2 * C + n + 1) * P],
                                               h16[:, q, n * P:(n + 1) * P], ident16[:, :])
                    ins.then_inc(h16T_ps, 1)
                if batch(s):
                    transposes(s, (0, 1))
                if batch(s - 1):
                    pe.wait_ge(state_ok, s)
                    for q in range(TPB):
                        for c in range(C):
                            ins = pe.matmul(bank[2][:, q * D:(q + 1) * D], st[:, c, q * P:(q + 1) * P],
                                            wa_T[:, 1, c, :], start=(c == 0), stop=(c == C - 1))
                    ins.then_inc(attn_ps, 1)
                if batch(s):
                    transposes(s, (2,))
                    pe.wait_ge(hT_ok, s + 1)
                    if isinstance(s, int) and s == 0:
                        pe.wait_ge(rows_ok, 1)
                    for e in range(C):
                        for c in range(C):
                            ins = pe.matmul(bank[1][:, e * S:(e + 1) * S], wa_T[:, 0, c, e * P:(e + 1) * P],
                                            hT[:, c, :], start=(c == 0), stop=(c == C - 1))
                    ins.then_inc(proj_ps, 1)
                    transposes(s, range(3, UNITS - 1))
                if batch(s - 3):
                    pe.wait_ge(h16T_ok, s - 2)
                    for q in range(TPB):
                        for n, (c, (a, m)) in enumerate((c, p) for c in range(C) for p in PARTS):
                            ins = pe.matmul(bank[4][:, q * E:(q + 1) * E], h16T[:, q, a * C + c, :],
                                            rt_T[:, c, m, :], start=(n == 0), stop=(n == 3 * C - 1))
                    ins.then_inc(logit_ps, 1)
                if batch(s):
                    transposes(s, (UNITS - 1,))

            mixer_steps(pe, body)

            pe.wait_ge(r_picked, 1)
            for t in range(NT):
                ins = pe.matmul(bank[1][:, 0:E], ones16[:, :], picked[:, t, :], start=(t == 0), stop=(t == NT - 1))
            ins.then_inc(count_ps, 1)
            flat = picked[:, :, :].rearrange("p t e -> p (t e)")
            pe.matmul(bank[0][:, :], before16[:, :], flat, start=True, stop=False)
            for t in range(NT - 1):
                n = NT - 1 - t
                ins = pe.matmul(bank[0][:, (t + 1) * E:].rearrange("p (t e) -> p t e", e=E), ones16[:, :],
                                picked[:, t:t + 1, :].to_broadcast([P, n, E]), start=False, stop=(n == 1))
            ins.then_inc(rank_ps, 1)

            def slots(h, slot, first, last):
                pe.wait_ge(row_ok, h + 1)
                pe.wait_ge(token_ok, h + 1)
                for m in range(HK):
                    ins = pe.matmul(bank[2][:, 0:RT], row_hot[slot][:, :, m], tile_token[slot][:, :, m],
                                    start=(first and m == 0), stop=(last and m == HK - 1))
                ins.then_inc(hot_used, 1)

            hot_steps(slots)
            pe.wait_ge(te_ok, 1)
            pe.matmul(bank[3][0:1, 0:P], te_col[:, :], ident[:, :], start=True, stop=True).then_inc(te_ps, 1)
            pe.wait_ge(slots_ok, 1)
            pe.wait_ge(route_ok, 1)

            HALF = U // 2
            regs = [[pe.alloc_register(f"tile_expert{h}_{n}") for n in range(U + G)] for h in range(2)]

            def load_experts(h, i):
                pe.load(regs[h], tile_expert[0:1, ds(U * i + HALF * h, U + G)])

            load_experts(0, 0)

            def group(i):
                expert = {n: pe.snap(r, min_val=0, max_val=E) for n, r in enumerate(regs[0])}
                for q in range(STEPS):
                    if (now := pair(i, q, 0)) is not None:
                        j, slot, place, body = now
                        if not shared(i, j):
                            pe.wait_ge(gathered[place], 16 * G * body + 16 * G)
                        else:
                            pe.wait_ge(sh_rows[place], 16 * (body - RT // U) + 16)
                        for g in range(G):
                            for n in range(2 * C):
                                m = g * 2 * C + n
                                ins = pe.transpose(bank16[slot][:, m * P:(m + 1) * P],
                                                   xg[:, place, g, n * P:(n + 1) * P], ident16[:, :])
                        ins.then_inc(xT_ps, 1)
                    if (now := pair(i, q, 4)) is not None:
                        j, slot, place, body = now
                        pe.wait_ge(hidlo_ok, j + 1)
                        for g in range(G):
                            w = wdn[:, ds(expert[G * q + g], 1), :, :].rearrange("p a h d -> p (a h) d")
                            for n, (a, m) in enumerate(PARTS):
                                ins = pe.matmul(bank[6 + slot][:, g * D:(g + 1) * D], hidT[:, slot, a, g, :],
                                                w[:, m, :], start=(n == 0), stop=(n == 2))
                        ins.then_inc(y_ps, 1)
                    if (now := pair(i, q, 3)) is not None:
                        j, slot, place, body = now
                        pe.wait_ge(hid_ok, j + 1)
                        for g in range(G):
                            ins = pe.transpose(bank[4 + slot][:, g * P:(g + 1) * P], hid[:, slot, g, :], ident[:, :])
                        ins.then_inc(hidT_ps, 1)
                    if (now := pair(i, q, 1)) is not None:
                        j, slot, place, body = now
                        pe.wait_ge(xT_ok, j + 1)
                        for g in range(G):
                            w = wgu[:, ds(expert[U + G * (q - 1) + g], 1), :, :, :]\
                                .rearrange("p a c h n -> p (a c) h n")
                            for n, (c, (a, m)) in enumerate((c, p) for c in range(C) for p in PARTS):
                                ins = pe.matmul(bank[2 + slot][:, g * 2 * I:(g + 1) * 2 * I],
                                                xT[:, slot, g, a * C + c, :], w[:, c, m, :],
                                                start=(n == 0), stop=(n == 3 * C - 1))
                        ins.then_inc(gu_ps, 1)
                    if q == 0:
                        load_experts(1, i)
                    if q == STEPS // 2:
                        load_experts(0, i + 1)
                    if q == STEPS // 2 - 1:
                        expert = {HALF + n: pe.snap(r, min_val=0, max_val=E) for n, r in enumerate(regs[1])}

            pair_steps(pe, group)


_INS = ["L0_attn_x", "L0_attn_W_in", "L0_attn_W_out", "L0_attn_decay", "L0_attn_bias",
        "L0_ffn_router_w", "L0_ffn_expert_bias", "L0_ffn_gate_w", "L0_ffn_up_w", "L0_ffn_down_w",
        "L0_ffn_shared_gate_w", "L0_ffn_shared_up_w", "L0_ffn_shared_down_w", "L0_c", "L0_wmod"]


def kernel(**inputs):
    import numpy as _np
    import concourse.bacc as _bacc
    from concourse import mybir as _mybir
    from concourse.bass_utils import run_bass_kernel_spmd as _run

    nc = _bacc.Bacc("TRN2", target_bir_lowering=False, num_devices=1)
    arrays, args = {}, []
    for name in _INS:
        a = _np.ascontiguousarray(inputs[name])
        arrays[f"in_{name}_dram"] = a
        args.append(nc.dram_tensor(f"in_{name}_dram", a.shape, _mybir.dt.from_np(a.dtype), kind="ExternalInput").ap())
    o = nc.dram_tensor("out_0_dram", inputs["L0_attn_x"].shape, _mybir.dt.float32, kind="ExternalOutput").ap()
    adaln_block(nc, *args, o)
    r = _run(nc, [arrays], core_ids=[0])
    return r.results[0]["out_0_dram"]
```

```python
from contextlib import ExitStack

import concourse.bass as bass
from concourse import mybir

fp32 = mybir.dt.float32
fp16 = mybir.dt.float16
i32 = mybir.dt.int32
u32 = mybir.dt.uint32
ALU = mybir.AluOpType
ACT = mybir.ActivationFunctionType
AX = mybir.AxisListType
ds = bass.ds

P = 128
SPLIT = 256.0
CLAMP = 7.0
EPS = 1e-5
GATE_MIN = 0.25


def at_least(engine, semaphore, value):
    if isinstance(value, int) and value <= 0:
        return
    engine.wait_ge(semaphore, value)


def adaln_block(nc, x, w_in, w_out, decay, bias, router_w, expert_bias, gate_w, up_w, down_w,
                sh_gate, sh_up, sh_down, cond, wmod, out):
    B, S, D = x.shape
    E, I, _ = gate_w.shape
    K = 4
    T = B * S
    NT = T // P
    TPB = S // P
    C = D // P
    G = 2
    U = 8
    STEPS = U // G
    RT = -(-((T * K + E * (P - 1)) // P) // U) * U
    AT = RT + NT
    NM = 6
    GA, GAB, CB, SB, GB = range(5)
    NR = 5
    PAIRS = E // 2
    PPB = PAIRS // B
    HL = 2 * D
    DEPTH = 4
    CS = K
    HT = 2
    CU = 8

    x_t = x.rearrange("b s d -> (b s) d").rearrange("(t p) d -> p t d", p=P)
    out_t = out.rearrange("b s d -> (b s) d").rearrange("(t p) d -> p t d", p=P)
    mod_dram = nc.dram_tensor("mod_rows_dram", (B, NR * D), fp32, kind="Internal").ap()
    hid_dram = nc.dram_tensor("hidden_dram", (T, HL), fp16, kind="Internal").ap()
    y_dram = nc.dram_tensor("expert_out_dram", (RT * P, D), fp32, kind="Internal").ap()
    hid_t = hid_dram.rearrange("(t p) d -> p t d", p=P)
    y_t = y_dram.rearrange("(t p) d -> p t d", p=P)

    ctx = ExitStack()
    with ctx:
        def sb(name, shape, dt):
            return ctx.enter_context(nc.sbuf_tensor(name, shape, dt))

        def sem(name):
            return ctx.enter_context(nc.semaphore(name))

        xs = sb("xs", [P, NT, D], fp32)
        wgu = sb("wgu", [P, E + 1, C, 2, 2 * I], fp16)
        wdn = sb("wdn", [P, E + 1, 2, D], fp16)
        ident = sb("ident", [P, P], fp32)
        ident16 = sb("ident16", [P, P], fp16)
        iota_i = sb("iota_i", [P, P], i32)
        iota16 = sb("iota16", [P, P], fp16)
        part_i = sb("part_i", [P, 1], i32)
        part_f = sb("part_f", [P, 1], fp32)
        token_i = sb("token_i", [P, NT], i32)
        token_f = sb("token_f", [P, NT], fp32)
        before16 = sb("before16", [P, P], fp16)
        ones16 = sb("ones16", [P, P], fp16)
        eps_t = sb("eps_t", [P, 1], fp32)
        one_t = sb("one_t", [P, 1], fp32)
        ebias = sb("ebias", [P, E], fp32)
        logits = sb("logits", [P, NT, E], fp32)
        gate_b = sb("gate_b", [P, B, D], fp32)
        slot_of = sb("slot_of", [P, NT, K], i32)
        token_of = sb("token_of", [P, AT + 1], i32)
        weight = sb("weight", [P, NT, K], fp32)
        tile_expert = sb("tile_expert", [1, G * DEPTH + AT + 2 * U], i32)
        wmod_s = sb("wmod_s", [P, C, NM * D], fp32)
        c_s = sb("c_s", [B, D], fp32)
        cT = sb("cT", [P, C, B], fp32)
        bias8 = sb("bias8", [B, D], fp32)
        rows = sb("rows", [B, NR, D], fp32)
        rows_a = sb("rows_a", [B, 2, D], fp32)
        rows_b = sb("rows_b", [B, 2, D], fp32)
        modT = sb("modT", [P, 2 * C, B], fp32)
        dec = sb("dec", [C, P], fp32)
        keep = sb("keep", [P, C], fp32)
        omk = sb("omk", [P, C], fp32)
        wa_n = sb("wa_n", [P, 2, C, D], fp32)
        wa_k = sb("wa_k", [P, C, D], fp32)
        wa_T = sb("wa_T", [P, 2, C, D], fp32)
        rt_n = sb("rt_n", [E, D], fp32)
        rt_T = sb("rt_T", [P, C, 2, E], fp16)
        nat = sb("nat", [P, 2, 3, 2, D], fp32)
        nat_sh = sb("nat_sh", [P, 3, D], fp32)
        stats = sb("stats", [P, 2, 6], fp32)
        mv1 = sb("mv1", [P, NT, 2], fp32)
        sd1 = sb("sd1", [P, NT], fp32)
        rs1 = sb("rs1", [P, NT], fp32)
        nm1 = sb("nm1", [P, NT], fp32)
        bc = sb("bc", [P, 2, 2, D], fp32)
        bc_a, bc_b = bc[:, 0, :, :], bc[:, 1, :, :]
        mix_room = sb("mix_room", [P, 6, 2 * D], fp32)
        xh, gated, xh2, h2 = (mix_room[:, n, :].rearrange("p (q d) -> p q d", q=TPB) for n in range(4))
        hT, st = (mix_room[:, n, :].rearrange("p (c t) -> p c t", c=C) for n in (4, 5))
        stats2 = sb("stats2", [P, TPB, 6], fp32)
        mv2 = sb("mv2", [P, TPB, 2], fp32)
        sd2 = sb("sd2", [P, TPB], fp32)
        rs2 = sb("rs2", [P, TPB], fp32)
        nm2 = sb("nm2", [P, TPB], fp32)
        h16 = sb("h16", [P, TPB, HL], fp16)
        h16T = sb("h16T", [P, TPB, 2 * C, P], fp16)

        room = wmod_s[:, :, :].rearrange("p c n -> p (c n)")

        def routing_room(n):
            return room[:, n * NT * E:(n + 1) * NT * E].rearrange("p (t e) -> p t e", e=E)
        r0, r1, r2, r3, r4, score = (routing_room(n) for n in range(6))
        top_v = sb("top_v", [P, NT, 8], fp32)
        top_i = sb("top_i", [P, NT, 8], u32)
        top16 = sb("top16", [P, NT, K], fp16)
        chosen = sb("chosen", [P, NT, E, K], fp16)
        pairs16 = r3.bitcast(fp16).rearrange("p t (e k) -> p t e k", k=K // 2)
        picked = sb("picked", [P, NT, E], fp16)
        tiles_i = sb("tiles_i", [P, E], i32)
        tiles_f = sb("tiles_f", [P, E], fp32)
        last_tile = sb("last_tile", [P, E], fp32)
        first_tile = sb("first_tile", [P, E], fp32)
        slot_f = sb("slot_f", [P, NT, K], fp32)
        slot_tmp = sb("slot_tmp", [P, NT, K], i32)
        slot_tile = sb("slot_tile", [P, NT, K], fp16)
        slot_row = sb("slot_row", [P, NT, K], fp16)
        prob = sb("prob", [P, K, NT], fp32)
        prob_sum = sb("prob_sum", [P, NT], fp32)
        te_cmp = sb("te_cmp", [P, E], fp32)
        te_col = sb("te_col", [P, 1], fp32)
        HK = HT * K

        def hot_room(room16, columns):
            return room16.rearrange("p (c m) -> p c m", m=HK)[:, 0:columns, :]
        iota_rep = hot_room(mix_room[:, 0, :].bitcast(fp16), P)
        row_hot = [hot_room(mix_room[:, 1 + n, :].bitcast(fp16), P) for n in range(2)]
        tile_hot = [hot_room(mix_room[:, 3 + n, :].bitcast(fp16), RT) for n in range(2)]
        tile_token = [hot_room(r.bitcast(fp16), RT)
                      for r in (mix_room[:, 5, :], nat_sh[:, :, :].rearrange("p a d -> p (a d)"))]
        col = sb("col", [P, STEPS, G], i32)
        nat_rows = nat[:, :, :, :, :].rearrange("p a b c d -> p (a b c) d")
        xg = nat_rows[:, 0:U, :].rearrange("p u n -> p (u n)").bitcast(fp16)\
            .rearrange("p (u g n) -> p u g n", u=STEPS, g=G)
        hidT = room[:, 0:NT * E].bitcast(fp16).rearrange("p (u a g n) -> p u a g n", u=2, a=2, g=G)
        xT = bc[:, :, :, :].rearrange("p a b d -> p (a b d)").bitcast(fp16)\
            .rearrange("p (u g c t) -> p u g c t", u=2, g=G, c=2 * C)
        clip = mix_room[:, 0:2, :].rearrange("p u (g n) -> p u g n", g=G)
        yo = mix_room[:, 2:4, :].rearrange("p u (g n) -> p u g n", g=G)
        act_g = mix_room[:, 4, :].rearrange("p (u g n) -> p u g n", u=2, g=G)
        hid = mix_room[:, 5, :].rearrange("p (u g n) -> p u g n", u=2, g=G)
        free = wgu[:, 0:E, :, :, :].rearrange("p e c h n -> p (e c h n)").bitcast(fp32)\
            .rearrange("p (r d) -> p r d", d=D)
        yg = free[:, 0:CU * K, :].rearrange("p (u k) d -> p u k d", u=CU)
        acc = free[:, CU * K:CU * (K + 2), :]
        fin = free[:, CU * (K + 2):CU * (K + 2) + NT, :]

        bank = [ctx.enter_context(nc.psum_tensor(f"bank{n}", [P, 512], fp32)) for n in range(8)]
        bank16 = [b[:, :].bitcast(fp16) for b in bank]

        ld_cond, ld_decay, ld_wmod, ld_small, ld_attn, ld_shared = (
            sem(n) for n in ("ld_cond", "ld_decay", "ld_wmod", "ld_small", "ld_attn", "ld_shared"))
        XL = 4
        ld_x = [sem(f"ld_x{n}") for n in range(XL)]
        consts = sem("consts")
        consts2 = sem("consts2")
        c_act, cT_ps, cT_ok, mod_ps, rows_ok, modT_ps, modT_ok, keep_ok, rows_stored = (
            sem(n) for n in ("c_act", "cT_ps", "cT_ok", "mod_ps", "rows_ok", "modT_ps", "modT_ok",
                             "keep_ok", "rows_stored"))
        dve_step = sem("dve_step")
        w_ps, wa_ok, w_hi, w_lo = (sem(n) for n in ("w_ps", "wa_ok", "w_hi", "w_lo"))
        dec_ps, gates_step = sem("dec_ps"), sem("gates_step")
        ln1_var, ln1_sd, ln1_stat = (sem(n) for n in ("ln1_var", "ln1_sd", "ln1_stat"))
        nat_ld = [sem(f"nat_ld{n}") for n in range(2)]
        pair_ps, pair_hi, pair_lo = sem("pair_ps"), sem("pair_hi"), sem("pair_lo")
        xh_ok, xhT_ps, hT_ok, proj_ps, state_ok, attn_ps = (
            sem(n) for n in ("xh_ok", "xhT_ps", "hT_ok", "proj_ps", "state_ok", "attn_ps"))
        bcg_ld, bca_ld, bcb_ld, xb_ok, gated_ok, x2_ok, stat2_ok, var2_ok, sd2_ok, rs2_ok, nm2_ok = (
            sem(n) for n in ("bcg_ld", "bca_ld", "bcb_ld", "xb_ok", "gated_ok", "x2_ok", "stat2_ok",
                             "var2_ok", "sd2_ok", "rs2_ok", "nm2_ok"))
        xh2_ok, h2m_ok, h2_ok, h16hi_ok, h16lo_ok, h16T_ps, h16T_ok, logit_ps, logit_ok, hid_stored = (
            sem(n) for n in ("xh2_ok", "h2m_ok", "h2_ok", "h16hi_ok", "h16lo_ok", "h16T_ps",
                             "h16T_ok", "logit_ps", "logit_ok", "hid_stored"))
        gateb_ld = sem("gateb_ld")
        r_neg, r_exp, r_u, r_ln, r_sp, r_score, r_picked, count_ps, rank_ps, te_ok, te_ps = (
            sem(n) for n in ("r_neg", "r_exp", "r_u", "r_ln", "r_sp", "r_score", "r_picked",
                             "count_ps", "rank_ps", "te_ok", "te_ps"))
        iota_ok, row_ok, tile_ok, token_ok = (sem(n) for n in ("iota_ok", "row_ok", "tile_ok", "token_ok"))
        hot_used, slots_ok, route_ok = (
            sem(n) for n in ("hot_used", "slots_ok", "route_ok"))
        col_ok = sem("col_ok")
        gathered = [sem(f"gathered{n}") for n in range(STEPS)]
        xT_ps, xT_ok, gu_ps, clip_ok, silu_ok, hid_ok, hidT_ps, hidhi_ok, hidlo_ok, y_ps, y_ok = (
            sem(n) for n in ("xT_ps", "xT_ok", "gu_ps", "clip_ok", "silu_ok", "hid_ok", "hidT_ps",
                             "hidhi_ok", "hidlo_ok", "y_ps", "y_ok"))
        y_stored = [sem(f"y_stored{n}") for n in range(2)]
        yg_ld = [sem(f"yg_ld{n}") for n in range(CU)]
        sh_rows = [sem(f"sh_rows{n}") for n in range(STEPS)]
        shy_ok, shx_ok = sem("shy_ok"), sem("shx_ok")
        weight_ok, first_ok = sem("weight_ok"), sem("first_ok")
        comb_step, fin_ok = sem("comb_step"), sem("fin_ok")
        out_stored = sem("out_stored")

        block = ctx.enter_context(nc.Block())

        PARTS = ((0, 0), (0, 1), (1, 0))

        UNITS = 3 * PPB

        def mixer_steps(engine, body):
            for s in range(3):
                body(s)
            with engine.Fori(3, B - 1) as s:
                body(s)
            for s in range(B - 1, B + 3):
                body(s)

        def batch(b):
            return not isinstance(b, int) or 0 <= b < B

        def last_batch(b):
            return isinstance(b, int) and b == B - 1

        SPLIT_AT = TPB * (B - 2)
        SCORED = (slice(0, SPLIT_AT), slice(SPLIT_AT, NT))

        def pair_weights(s, u):
            first, j = 2 * (PPB * s + u // 3), u % 3
            if j < 2:
                return wgu[:, ds(first + j, 1), :, :, :].rearrange("p a c h n -> p (a c) h n"), j
            return wdn[:, ds(first, 2), :, :], j

        def rows_of(b):
            return xs[:, ds(TPB * b, TPB), :]

        def hot_steps(step):
            for h in range(NT // HT):
                step(h, h % 2, h == 0, h == NT // HT - 1)


        def pair_steps(engine, group):
            group(0)
            group(1)
            with engine.Fori(2, RT // U) as i:
                group(i)
            for i in range(RT // U, AT // U + 1):
                group(i)

        def pair(i, q, lag):
            body, place = i + (q - lag) // STEPS, (q - lag) % STEPS
            if isinstance(body, int) and not 0 <= body < AT // U:
                return None
            return STEPS * body + place, place % 2, place, body

        def shared(i, j):
            return isinstance(i, int) and j >= RT // G

        @block.sync
        def _(sp):
            sp.dma_start(c_s[:, :], cond).then_inc(ld_cond, 16)

            def load_x(n):
                a, b = n * NT // XL, (n + 1) * NT // XL
                sp.dma_start(xs[:, a:b, :], x_t[:, a:b, :]).then_inc(ld_x[n], 16)

            load_x(0)
            for w, src in enumerate((w_in, w_out)):
                sp.dma_start(wa_n[:, w, :, :], src.rearrange("(c p) d -> p c d", p=P)).then_inc(ld_attn, 16)
            for n in range(1, XL):
                load_x(n)
            sp.dma_start(nat_sh[:, 0, :], sh_gate).then_inc(ld_shared, 16)
            sp.dma_start(nat_sh[:, 1, :], sh_up).then_inc(ld_shared, 16)
            sp.dma_start(nat_sh[:, 2, :].rearrange("p (r i) -> p r i", i=I),
                         sh_down.rearrange("(r p) i -> p r i", p=P)).then_inc(ld_shared, 16)

            def load_pair(pair, slot):
                e = ds(2 * pair, 2)
                sp.dma_start(nat[:, slot, 0, :, :], gate_w[e, :, :].rearrange("e i d -> i e d"))\
                  .then_inc(nat_ld[slot], 16)
                sp.dma_start(nat[:, slot, 1, :, :], up_w[e, :, :].rearrange("e i d -> i e d"))\
                  .then_inc(nat_ld[slot], 16)
                for j in range(2):
                    sp.dma_start(nat[:, slot, 2, j, :].rearrange("p (r i) -> p r i", i=I),
                                 down_w[ds(2 * pair + j, 1), :, :].rearrange("e (r p) i -> p (e r) i", p=P))\
                      .then_inc(nat_ld[slot], 16)

            for h in range(2):
                load_pair(h, h)
            def next_first_pair(s):
                sp.wait_ge(pair_ps, UNITS * s + 3)
                load_pair(PPB * (s + 1), 0)

            sp.wait_ge(rows_ok, 1)
            sp.dma_start(mod_dram, rows[:, :, :].rearrange("b r d -> b (r d)")).then_inc(rows_stored, 16)
            next_first_pair(0)
            sp.wait_ge(rows_stored, 16)
            mod_v = mod_dram.rearrange("b (r d) -> b r d", d=D)

            def load_rows(dst, b, first, semaphore):
                sp.dma_start(dst[:, :, :], mod_v[ds(b, 1), first:first + 2, :].to_broadcast([P, 2, D]))\
                  .then_inc(semaphore, 16)

            def load_row(n, b, row, semaphore):
                sp.dma_start(bc_a[:, n:n + 1, :], mod_v[ds(b, 1), row:row + 1, :].to_broadcast([P, 1, D]))\
                  .then_inc(semaphore, 16)

            load_row(1, 0, GAB, bca_ld)
            load_row(0, 0, GA, bcg_ld)
            load_rows(bc_b, 0, CB, bcb_ld)

            def body(s):
                if batch(s) and batch(s + 1):
                    if not (isinstance(s, int) and s == 0):
                        next_first_pair(s)
                    sp.wait_ge(xb_ok, s + 1)
                    load_row(1, s + 1, GAB, bca_ld)
                if batch(s) and batch(s - 1):
                    sp.wait_ge(gated_ok, s)
                    load_row(0, s, GA, bcg_ld)
                if batch(s - 2) and batch(s - 1):
                    sp.wait_ge(h2_ok, s - 1)
                    load_rows(bc_b, s - 1, CB, bcb_ld)
                if batch(s) and batch(s + 1):
                    for h in range(1, PPB):
                        sp.wait_ge(pair_ps, UNITS * s + 3 * h + 3)
                        load_pair(PPB * (s + 1) + h, h)
                if batch(s - 2):
                    sp.wait_ge(h16lo_ok, s - 1)
                    sp.dma_start(hid_t[:, ds(TPB * (s - 2), TPB), :], h16[:, :, :]).then_inc(hid_stored, 16)

            mixer_steps(sp, body)
            for b in range(B):
                sp.dma_start(gate_b[:, b:b + 1, :], mod_v[b:b + 1, GB:GB + 1, :].to_broadcast([P, 1, D]))\
                  .then_inc(gateb_ld, 16)

            def store_y(j, slot):
                sp.wait_ge(y_ok, j + 1)
                sp.dma_start(y_t[:, ds(G * j, G), :], yo[:, slot, :, :]).then_inc(y_stored[slot], 16)

            def load_shared(j):
                sp.wait_ge(xT_ps, j - STEPS + 1)
                t = G * j - RT
                sp.dma_start(xg[:, j % STEPS, :, :], hid_t[:, t:t + G, :]).then_inc(sh_rows[j % STEPS], 16)

            RPAIRS, APAIRS = RT // G, AT // G
            AHEAD = STEPS + DEPTH + 1
            looped = (RPAIRS - AHEAD) // 2
            sp.wait_ge(hid_stored, 16 * B)
            with sp.Fori(0, looped) as i:
                for slot in range(2):
                    store_y(2 * i + slot, slot)
            for j in range(2 * looped, RPAIRS):
                store_y(j, j % 2)
                if RPAIRS <= j + AHEAD < APAIRS:
                    load_shared(j + AHEAD)
            for slot in range(2):
                sp.wait_ge(y_stored[slot], 16 * (RPAIRS // 2))

            with sp.Fori(0, NT) as t:
                sp.wait_ge(fin_ok, t + 1)
                sp.dma_start(out_t[:, ds(t, 1), :], fin[:, ds(t, 1), :]).then_inc(out_stored, 16)
            sp.wait_ge(out_stored, 16 * NT)

        @block.gpsimd
        def _(pool):
            pool.memset(ident[:, :], 0.0).then_inc(consts, 1)
            pool.iota(iota_i[:, :], pattern=[[1, P]], base=0, channel_multiplier=0).then_inc(consts, 1)
            pool.iota(part_i[:, :], pattern=[[0, 1]], base=0, channel_multiplier=1).then_inc(consts, 1)
            pool.iota(token_i[:, :], pattern=[[P, NT]], base=0, channel_multiplier=1).then_inc(consts, 1)
            pool.memset(ones16[:, :], 1.0).then_inc(consts, 1)
            pool.memset(eps_t[:, :], EPS).then_inc(consts, 1)
            pool.memset(one_t[:, :], 1.0).then_inc(consts, 1)
            pool.memset(tile_expert[:, :], E).then_inc(consts, 1)
            pool.memset(token_of[:, AT:AT + 1], 0).then_inc(consts, 1)
            pool.wait_ge(consts, 9)
            pool.affine_select(out=ident[:, :], in_=ident[:, :], compare_op=ALU.not_equal, fill=1.0,
                               base=0, pattern=[[-1, P]], channel_multiplier=1).then_inc(consts, 1)

            def body(s):
                if batch(s):
                    pool.wait_ge(xh_ok, s + 1)
                    pool.wait_ge(bca_ld, 16 * s + 16)
                    pool.tensor_tensor(rows_of(s), rows_of(s), bc_a[:, 1:2, :].to_broadcast([P, TPB, D]), ALU.add)\
                        .then_inc(xb_ok, 1)
                b = s - 2
                if batch(b) and not last_batch(b):
                    pool.wait_ge(xh2_ok, b + 1)
                    pool.wait_ge(bcb_ld, 16 * b + 16)
                    at_least(pool, h16lo_ok, b)
                    pool.tensor_tensor(h2, xh2, bc_b[:, 0:1, :].to_broadcast([P, TPB, D]), ALU.mult)\
                        .then_inc(h2m_ok, 1)
                    pool.wait_ge(h2m_ok, b + 1)
                    pool.tensor_tensor(h2, h2, bc_b[:, 1:2, :].to_broadcast([P, TPB, D]), ALU.add)\
                        .then_inc(h2_ok, 1)
                    pool.wait_ge(h16hi_ok, b + 1)
                    pool.tensor_tensor(h16[:, :, D:HL], h2, h16[:, :, 0:D], ALU.subtract).then_inc(h16lo_ok, 1)

            mixer_steps(pool, body)

            pool.wait_ge(consts2, 4)
            pool.wait_ge(xhT_ps, B)
            pool.tensor_copy(iota_rep, iota16[:, :].rearrange("p (c m) -> p c m", m=1).to_broadcast([P, P, HK]))\
                .then_inc(iota_ok, 1)

            pool.wait_ge(slots_ok, 1)
            pool.wait_ge(hid_stored, 16 * B)

            def copy_column(j, place):
                pool.tensor_copy(col[:, place, :], token_of[:, ds(G * j, G)]).then_inc(col_ok, 1)

            def group(i):
                for q in range(STEPS):
                    now = pair(i, q, 0)
                    if now is None or shared(i, now[0]):
                        continue
                    j, slot, place, body = now
                    at_least(pool, xT_ps, j - STEPS + 1)
                    pool.wait_ge(col_ok, j + 1)
                    j_next, _, place_next, body_next = pair(i, q, -1)
                    at_least(pool, gathered[place_next], 16 * G * body_next)
                    copy_column(j_next, place_next)
                    for g in range(G):
                        pool.indirect_dma_start(xg[:, place, g, :], None, hid_dram,
                                                bass.IndirectOffsetOnAxis(ap=col[:, place, g:g + 1], axis=0))\
                            .then_inc(gathered[place], 16)

            copy_column(0, 0)
            pair_steps(pool, group)

            for slot in range(2):
                pool.wait_ge(y_stored[slot], 16 * (RT // G // 2))

            for t in range(NT):
                at_least(pool, comb_step, CS * (t - CU) + K - 1)
                for k in range(K):
                    pool.indirect_dma_start(yg[:, t % CU, k, :], None, y_dram,
                                            bass.IndirectOffsetOnAxis(ap=slot_of[:, t, k:k + 1], axis=0))\
                        .then_inc(yg_ld[t % CU], 16)

        @block.scalar
        def _(act):
            act.dma_start(dec[:, :], decay.rearrange("(c p) -> c p", p=P)).then_inc(ld_decay, 16)
            act.dma_start(wmod_s[:, :, :], wmod.rearrange("(c p) n -> p c n", p=P)).then_inc(ld_wmod, 16)
            act.dma_start(bias8[:, :], bias.rearrange("(a d) -> a d", a=1).to_broadcast([B, D])).then_inc(ld_small, 16)
            act.dma_start(rt_n[:, :], router_w).then_inc(ld_small, 16)
            act.dma_start(ebias[:, :], expert_bias.rearrange("(a e) -> a e", a=1).to_broadcast([P, E]))\
               .then_inc(ld_small, 16)
            act.wait_ge(ld_cond, 16)
            act.activation(c_s[:, :], c_s[:, :], ACT.Silu).then_inc(c_act, 1)
            act.wait_ge(ld_decay, 16)
            act.activation(dec[:, :], dec[:, :], ACT.Sigmoid).then_inc(keep_ok, 1)

            act.wait_ge(ln1_var, NT)
            act.activation(sd1[:, :], mv1[:, :, 1], ACT.Sqrt, bias=eps_t[:, :]).then_inc(ln1_sd, 1)

            for w in range(2):
                act.wait_ge(w_ps, w + 1)
                act.activation(wa_T[:, w, :, :], bank[(7, 4)[w]][:, :].rearrange("p (c e) -> p c e", c=C), ACT.Copy)\
                   .then_inc(wa_ok, 1)

            act.wait_ge(w_ps, 3)
            act.activation(rt_T[:, :, 0, :], bank[6][:, D:D + C * E].rearrange("p (c e) -> p c e", e=E),
                           ACT.Copy, scale=SPLIT).then_inc(w_hi, 1)
            act.activation(wdn[:, E, 0, :], bank[6][:, 0:D], ACT.Copy, scale=SPLIT).then_inc(w_hi, 1)
            act.wait_ge(w_ps, 4)
            act.activation(wgu[:, E, :, 0, :], bank[5][:, :].rearrange("p (c n) -> p c n", c=C),
                           ACT.Copy, scale=SPLIT).then_inc(w_hi, 1)

            def hi_half(s, u):
                act.wait_ge(pair_ps, UNITS * s + u + 1)
                w, j = pair_weights(s, u)
                act.activation(w[:, :, 0, :], bank[5 + j][:, :].rearrange("p (c n) -> p c n", c=2),
                               ACT.Copy, scale=SPLIT).then_inc(pair_hi, 1)

            def score_exp(n):
                act.wait_ge(r_neg, n + 1)
                act.activation(r1[:, SCORED[n], :], r0[:, SCORED[n], :], ACT.Exp).then_inc(r_exp, 1)

            def score_log(n):
                act.wait_ge(r_u, n + 1)
                act.activation(r3[:, SCORED[n], :], r2[:, SCORED[n], :], ACT.Ln).then_inc(r_ln, 1)

            def score_root(n):
                act.wait_ge(r_sp, n + 1)
                act.activation(score[:, SCORED[n], :], r4[:, SCORED[n], :], ACT.Sqrt).then_inc(r_score, 1)

            def body(s):
                if batch(s):
                    act.wait_ge(xhT_ps, s + 1)
                    if isinstance(s, int) and s == 0:
                        act.wait_ge(modT_ok, 2)
                    for c in range(C):
                        ins = act.activation(hT[:, c, :], bank[0][:, c * S:(c + 1) * S], ACT.Identity,
                                             scale=modT[:, C + c, ds(s, 1)], bias=modT[:, c, ds(s, 1)])
                    ins.then_inc(hT_ok, 1)
                    hi_half(s, 0)
                if batch(s - 2) and not last_batch(s - 2):
                    act.wait_ge(nm2_ok, s - 1)
                    for q in range(TPB):
                        ins = act.activation(xh2[:, q, :], xs[:, ds(TPB * (s - 2) + q, 1), :]
                                             .rearrange("p a d -> p (a d)"), ACT.Identity,
                                             scale=rs2[:, q:q + 1], bias=nm2[:, q:q + 1])
                    ins.then_inc(xh2_ok, 1)
                if batch(s):
                    hi_half(s, 1)
                if last_batch(s - 2):
                    score_exp(0)
                if batch(s - 3):
                    act.wait_ge(h16T_ps, s - 2)
                    act.activation(h16T[:, :, :, :].rearrange("p q c t -> p (q c t)"), bank16[3], ACT.Copy)\
                       .then_inc(h16T_ok, 1)
                if batch(s):
                    hi_half(s, 2)
                if batch(s - 2):
                    at_least(act, hid_stored, 16 * (s - 2))
                    act.wait_ge(h2_ok, s - 1)
                    act.activation(h16[:, :, 0:D], h2, ACT.Copy).then_inc(h16hi_ok, 1)
                if last_batch(s - 2):
                    score_log(0)
                if batch(s):
                    for u in range(3, UNITS - 1):
                        hi_half(s, u)
                if batch(s - 1):
                    act.wait_ge(var2_ok, s)
                    act.activation(sd2[:, :], mv2[:, :, 1], ACT.Sqrt, bias=eps_t[:, :]).then_inc(sd2_ok, 1)
                if last_batch(s - 3):
                    score_root(0)
                elif batch(s - 3):
                    act.wait_ge(logit_ps, s - 2)
                    act.activation(logits[:, ds(TPB * (s - 3), TPB), :],
                                   bank[4][:, 0:TPB * E].rearrange("p (q e) -> p q e", e=E),
                                   ACT.Copy, scale=1.0 / SPLIT).then_inc(logit_ok, 1)
                if batch(s):
                    hi_half(s, UNITS - 1)

            mixer_steps(act, body)

            score_exp(1)
            score_log(1)
            score_root(1)

            def token_step(h, slot, first, last):
                act.wait_ge(tile_ok, h + 1)
                at_least(act, hot_used, h - 1)
                for u in range(HT):
                    m = slice(u * K, (u + 1) * K)
                    ins = act.activation(tile_token[slot][:, :, m], tile_hot[slot][:, :, m], ACT.Copy,
                                         scale=token_f[:, ds(HT * h + u, 1)])
                ins.then_inc(token_ok, 1)

            hot_steps(token_step)

            def group(i):
                for q in range(STEPS):
                    if (now := pair(i, q, 3)) is not None:
                        j, slot, place, body = now
                        act.wait_ge(hidT_ps, j + 1)
                        act.activation(hidT[:, slot, 0, :, :].rearrange("p g n -> p (g n)"),
                                       bank[4 + slot][:, 0:G * P], ACT.Copy).then_inc(hidhi_ok, 1)
                    if (now := pair(i, q, 0)) is not None:
                        j, slot, place, body = now
                        act.wait_ge(xT_ps, j + 1)
                        act.activation(xT[:, slot, :, :, :].rearrange("p g c t -> p (g c t)"),
                                       bank16[slot], ACT.Copy).then_inc(xT_ok, 1)
                    if (now := pair(i, q, 1)) is not None:
                        j, slot, place, body = now
                        act.wait_ge(clip_ok, j + 1)
                        act.activation(act_g[:, slot, :, :], clip[:, slot, :, 0:I], ACT.Silu, scale=1.0 / SPLIT)\
                           .then_inc(silu_ok, 1)

            pair_steps(act, group)

            act.wait_ge(weight_ok, 1)
            with act.Fori(0, NT // CU) as i:
                for u in range(CU):
                    t = CU * i + u
                    act.wait_ge(yg_ld[u], 16 * K * i + 16 * K)
                    act.activation(fin[:, ds(t, 1), :].rearrange("p a d -> p (a d)"), yg[:, u, 0, :], ACT.Copy,
                                   scale=weight[:, ds(t, 1), 0:1].rearrange("p a k -> p (a k)"))\
                       .then_inc(first_ok, 1)

        @block.vector
        def _(dve):
            steps = [0]

            def then(ins):
                steps[0] += 1
                ins.then_inc(dve_step, 1)
                dve.wait_ge(dve_step, steps[0])

            dve.wait_ge(consts, 10)
            dve.tensor_copy(part_f[:, :], part_i[:, :]).then_inc(consts2, 1)
            dve.tensor_copy(token_f[:, :], token_i[:, :]).then_inc(consts2, 1)
            dve.tensor_copy(ident16[:, :], ident[:, :]).then_inc(consts2, 1)
            dve.tensor_copy(iota16[:, :], iota_i[:, :]).then_inc(consts2, 1)
            dve.tensor_copy(token_of[:, RT:AT], token_i[:, :]).then_inc(consts2, 1)
            dve.wait_ge(consts2, 5)
            dve.tensor_scalar(before16[:, :], iota16[:, :], part_f[:, :], None, ALU.is_gt).then_inc(consts2, 1)

            dve.wait_ge(cT_ps, 1)
            dve.tensor_copy(cT[:, :, :], bank[0][:, 0:C * B].rearrange("p (c b) -> p c b", b=B)).then_inc(cT_ok, 1)
            dve.wait_ge(dec_ps, 1)
            then(dve.tensor_copy(keep[:, :], bank[3][:, 0:C]))
            then(dve.tensor_scalar(omk[:, :], keep[:, :], -1.0, 1.0, ALU.mult, ALU.add))

            def ln1_statistics(t):
                for q in range(2):
                    if t:
                        dve.wait_ge(ln1_var, t + q - 1)
                    dve.bn_stats(stats[:, q, :], xs[:, t + q, :]).then_inc(ln1_stat, 1)
                for q in range(2):
                    dve.wait_ge(ln1_stat, t + q + 1)
                    dve.bn_aggr(mv1[:, t + q, :], stats[:, q, :]).then_inc(ln1_var, 1)

            for n in range(XL):
                dve.wait_ge(ld_x[n], 16)
                for t in range(n * NT // XL, (n + 1) * NT // XL, 2):
                    ln1_statistics(t)
                if n == 0:
                    dve.wait_ge(ld_attn, 32)
                    for c in range(C):
                        dve.tensor_scalar(wa_k[:, c, :], wa_n[:, 0, c, :], omk[:, c:c + 1], None, ALU.mult)\
                           .then_inc(keep_ok, 1)
            dve.wait_ge(modT_ps, 1)
            dve.tensor_copy(modT[:, 0:C, :], bank[3][:, 64:64 + C * B].rearrange("p (c b) -> p c b", b=B))\
               .then_inc(modT_ok, 1)
            dve.tensor_scalar(modT[:, C:2 * C, :], bank[3][:, 64 + C * B:64 + 2 * C * B]
                              .rearrange("p (c b) -> p c b", b=B), 1.0, None, ALU.add).then_inc(modT_ok, 1)
            dve.wait_ge(mod_ps, 1)
            for n, (bk, half) in enumerate(((1, 0), (2, 1))):
                g = bank[bk][0:B, half * D:(half + 1) * D]
                dve.tensor_scalar(rows_a[:, n, :], g, 0.0, 2.0, ALU.is_ge, ALU.mult).then_inc(gates_step, 1)
            dve.tensor_copy(rows[:, SB, :], bank[1][0:B, D:2 * D])
            dve.tensor_scalar(rows[:, CB, :], bank[2][0:B, 0:D], 1.0, None, ALU.add)
            dve.wait_ge(ln1_sd, 1)
            then(dve.reciprocal(rs1[:, :], sd1[:, :]))
            then(dve.scalar_tensor_tensor(nm1[:, :], mv1[:, :, 0], -1.0, rs1[:, :], ALU.mult, ALU.mult))

            def normalise(b):
                for q in range(TPB):
                    t = TPB * b + q
                    ins = dve.tensor_scalar(xh[:, q, :], xs[:, ds(t, 1), :].rearrange("p a d -> p (a d)"),
                                            rs1[:, ds(t, 1)], nm1[:, ds(t, 1)], ALU.mult, ALU.add)
                ins.then_inc(xh_ok, 1)

            normalise(0)

            dve.wait_ge(w_hi, 2)
            dve.scalar_tensor_tensor(rt_T[:, :, 1, :], bank[6][:, D:D + C * E].rearrange("p (c e) -> p c e", e=E),
                                     SPLIT, rt_T[:, :, 0, :], ALU.mult, ALU.subtract).then_inc(w_lo, 1)
            dve.scalar_tensor_tensor(wdn[:, E, 1, :], bank[6][:, 0:D], SPLIT, wdn[:, E, 0, :],
                                     ALU.mult, ALU.subtract).then_inc(w_lo, 1)
            dve.wait_ge(w_hi, 3)
            dve.scalar_tensor_tensor(wgu[:, E, :, 1, :], bank[5][:, :].rearrange("p (c n) -> p c n", c=C),
                                     SPLIT, wgu[:, E, :, 0, :], ALU.mult, ALU.subtract).then_inc(w_lo, 1)

            dve.wait_ge(gates_step, 2)
            then(dve.tensor_scalar(rows_a[:, :, :], rows_a[:, :, :], -1.0, None, ALU.add))
            for n, (bk, half) in enumerate(((1, 0), (2, 1))):
                ins = dve.tensor_tensor(rows_b[:, n, :], bank[bk][0:B, half * D:(half + 1) * D], rows_a[:, n, :],
                                        ALU.mult)
            then(ins)
            for n, r in enumerate((GA, GB)):
                ins = dve.scalar_tensor_tensor(rows[:, r, :], rows_b[:, n, :], GATE_MIN, rows_a[:, n, :],
                                               ALU.max, ALU.mult)
            then(ins)
            dve.wait_ge(ld_small, 48)
            dve.tensor_tensor(rows[:, GAB, :], rows[:, GA, :], bias8[:, :], ALU.mult).then_inc(rows_ok, 1)

            def routing_neg(n):
                c, lg = SCORED[n], logits[:, SCORED[n], :]
                dve.scalar_tensor_tensor(r0[:, c, :], lg, -1.0, lg, ALU.mult, ALU.min).then_inc(r_neg, 1)

            def routing_u(n):
                c = SCORED[n]
                dve.wait_ge(r_exp, n + 1)
                dve.tensor_scalar(r2[:, c, :], r1[:, c, :], 1.0, None, ALU.add).then_inc(r_u, 1)

            def routing_softplus(n):
                c, lg = SCORED[n], logits[:, SCORED[n], :]
                dve.wait_ge(r_u, n + 1)
                then(dve.scalar_tensor_tensor(r4[:, c, :], r2[:, c, :], -1.0, r1[:, c, :],
                                              ALU.add, ALU.subtract))
                then(dve.scalar_tensor_tensor(r0[:, c, :], lg, 0.0, r4[:, c, :], ALU.max, ALU.subtract))
                dve.wait_ge(r_ln, n + 1)
                dve.tensor_tensor(r4[:, c, :], r3[:, c, :], r0[:, c, :], ALU.add).then_inc(r_sp, 1)

            def routing_best(n, what):
                c = SCORED[n]
                tiles, nt = range(c.start, c.stop), c.stop - c.start
                if "values" in what:
                    dve.wait_ge(r_score, n + 1)
                    then(dve.tensor_tensor(r2[:, c, :], score[:, c, :],
                                           ebias[:, :].rearrange("p (a e) -> p a e", a=1)
                                           .to_broadcast([P, nt, E]), ALU.add))
                    for t in tiles:
                        ins = dve.max(top_v[:, t, :], r2[:, t, :])
                    then(ins)
                if "indices" in what:
                    for t in tiles:
                        ins = dve.max_index(top_i[:, t, :], top_v[:, t, :], r2[:, t, :])
                    then(ins)
                if "choices" in what:
                    then(dve.tensor_copy(top16[:, c, :], top_i[:, c, 0:K]))
                    dve.wait_ge(iota_ok, 1)
                    then(dve.tensor_tensor(
                        chosen[:, c, :, :], iota_rep[:, 0:E, 0:K].rearrange("p (a e) k -> p a e k", a=1)
                        .to_broadcast([P, nt, E, K]),
                        top16[:, c, :].rearrange("p t (a k) -> p t a k", a=1).to_broadcast([P, nt, E, K]),
                        ALU.is_equal))
                    then(dve.tensor_tensor(pairs16[:, c, :, :], chosen[:, c, :, 0:K // 2], chosen[:, c, :, K // 2:K],
                                           ALU.add))
                    dve.tensor_tensor(picked[:, c, :], pairs16[:, c, :, 0], pairs16[:, c, :, 1], ALU.add)\
                       .then_inc(r_picked, 1)

            def lo_half(s, u):
                dve.wait_ge(pair_hi, UNITS * s + u + 1)
                w, j = pair_weights(s, u)
                dve.scalar_tensor_tensor(w[:, :, 1, :], bank[5 + j][:, :].rearrange("p (c n) -> p c n", c=2),
                                         SPLIT, w[:, :, 0, :], ALU.mult, ALU.subtract).then_inc(pair_lo, 1)

            def body(s):
                if batch(s - 2):
                    dve.wait_ge(sd2_ok, s - 1)
                    dve.reciprocal(rs2[:, :], sd2[:, :]).then_inc(rs2_ok, 1)
                    dve.wait_ge(rs2_ok, s - 1)
                    dve.scalar_tensor_tensor(nm2[:, :], mv2[:, :, 0], -1.0, rs2[:, :], ALU.mult, ALU.mult)\
                       .then_inc(nm2_ok, 1)
                if last_batch(s - 2):
                    b = B - 1
                    dve.wait_ge(nm2_ok, b + 1)
                    dve.wait_ge(h2m_ok, b)
                    for q in range(TPB):
                        ins = dve.tensor_scalar(xh2[:, q, :], xs[:, TPB * b + q, :], rs2[:, q:q + 1],
                                                nm2[:, q:q + 1], ALU.mult, ALU.add)
                    ins.then_inc(xh2_ok, 1)
                    dve.wait_ge(logit_ok, B - 2)
                    routing_neg(0)
                    dve.wait_ge(xh2_ok, b + 1)
                    dve.wait_ge(bcb_ld, 16 * b + 16)
                    dve.wait_ge(h16lo_ok, b)
                    dve.tensor_tensor(h2, xh2, bc_b[:, 0:1, :].to_broadcast([P, TPB, D]), ALU.mult)\
                       .then_inc(h2m_ok, 1)
                    dve.wait_ge(h2m_ok, b + 1)
                    dve.tensor_tensor(h2, h2, bc_b[:, 1:2, :].to_broadcast([P, TPB, D]), ALU.add)\
                       .then_inc(h2_ok, 1)
                    routing_u(0)
                    dve.wait_ge(h16hi_ok, b + 1)
                    dve.tensor_tensor(h16[:, :, D:HL], h2, h16[:, :, 0:D], ALU.subtract).then_inc(h16lo_ok, 1)
                    routing_softplus(0)
                if last_batch(s - 3):
                    dve.wait_ge(logit_ps, B)
                    dve.wait_ge(logit_ok, B - 1)
                    dve.tensor_scalar(logits[:, TPB * (B - 1):NT, :],
                                      bank[4][:, 0:TPB * E].rearrange("p (q e) -> p q e", e=E),
                                      1.0 / SPLIT, None, ALU.mult).then_inc(logit_ok, 1)
                    dve.wait_ge(logit_ok, B)
                    routing_neg(1)
                if batch(s) and batch(s + 1):
                    dve.wait_ge(xhT_ps, s + 1)
                    normalise(s + 1)
                if batch(s - 1):
                    lo_half(s - 1, UNITS - 1)
                if batch(s):
                    lo_half(s, 0)
                if batch(s - 1):
                    dve.wait_ge(attn_ps, s)
                    dve.wait_ge(bcg_ld, 16 * s)
                    dve.tensor_tensor(gated, bank[2][:, :].rearrange("p (q d) -> p q d", q=TPB),
                                      bc_a[:, 0:1, :].to_broadcast([P, TPB, D]), ALU.mult).then_inc(gated_ok, 1)
                if batch(s):
                    lo_half(s, 1)
                if batch(s - 1):
                    dve.wait_ge(xb_ok, s)
                    dve.wait_ge(gated_ok, s)
                    dve.tensor_tensor(rows_of(s - 1), rows_of(s - 1), gated, ALU.add).then_inc(x2_ok, 1)
                    dve.wait_ge(x2_ok, s)
                if batch(s):
                    lo_half(s, 2)
                if batch(s - 1):
                    for q in range(TPB):
                        ins = dve.bn_stats(stats2[:, q, :], xs[:, ds(TPB * (s - 1) + q, 1), :]
                                           .rearrange("p a d -> p (a d)"))
                    ins.then_inc(stat2_ok, 1)
                    dve.wait_ge(stat2_ok, s)
                if batch(s):
                    dve.wait_ge(proj_ps, s + 1)
                    for c in range(C):
                        ins = dve.tensor_tensor_scan(st[:, c, :], keep[:, c:c + 1].to_broadcast([P, S]),
                                                     bank[1][:, c * S:(c + 1) * S], 0.0, ALU.mult, ALU.add)
                    ins.then_inc(state_ok, 1)
                if batch(s - 1):
                    for q in range(TPB):
                        ins = dve.bn_aggr(mv2[:, q, :], stats2[:, q, :])
                    ins.then_inc(var2_ok, 1)
                if batch(s):
                    for u in range(3, UNITS - 1):
                        lo_half(s, u)

            mixer_steps(dve, body)

            routing_best(0, ("values",))
            routing_u(1)
            routing_best(0, ("indices",))
            routing_softplus(1)
            routing_best(0, ("choices",))
            routing_best(1, ("values", "indices", "choices"))
            dve.wait_ge(count_ps, 1)
            then(dve.tensor_scalar(tiles_i[:, :], bank[1][:, 0:E], float(P - 1), None, ALU.add))
            then(dve.tensor_scalar(tiles_i[:, :], tiles_i[:, :], 7, None, ALU.logical_shift_right))
            then(dve.tensor_copy(tiles_f[:, :], tiles_i[:, :]))
            then(dve.tensor_tensor_scan(last_tile[:, :], one_t[:, :].to_broadcast([P, E]), tiles_f[:, :], 0.0,
                                        ALU.mult, ALU.add))
            then(dve.tensor_tensor(first_tile[:, :], last_tile[:, :], tiles_f[:, :], ALU.subtract))
            dve.wait_ge(rank_ps, 1)
            then(dve.scalar_tensor_tensor(
                r0, first_tile[:, :].rearrange("p (a e) -> p a e", a=1).to_broadcast([P, NT, E]), float(P),
                bank[0][:, :].rearrange("p (t e) -> p t e", e=E), ALU.mult, ALU.add))
            then(dve.scalar_tensor_tensor(r1, r0, 1.0, picked[:, :, :], ALU.add, ALU.mult))
            for t in range(NT):
                ins = dve.max(top_v[:, t, :], r1[:, t, :])
            then(ins)
            dve.tensor_scalar(slot_f[:, :, :], top_v[:, :, 0:K], -1.0, None, ALU.add)
            then(dve.tensor_scalar(slot_of[:, :, :], top_v[:, :, 0:K], -1.0, None, ALU.add))
            then(dve.tensor_scalar(slot_tmp[:, :, :], slot_of[:, :, :], 7, None, ALU.logical_shift_right))
            dve.tensor_copy(slot_tile[:, :, :], slot_tmp[:, :, :])
            then(dve.scalar_tensor_tensor(slot_row[:, :, :], slot_tmp[:, :, :], -float(P), slot_f[:, :, :],
                                          ALU.mult, ALU.add))

            def hots(h, slot, first, last):
                def equal(hot, of, columns):
                    v = of[:, ds(HT * h, HT), :].rearrange("p (a t) k -> p a (t k)", a=1)
                    return dve.tensor_tensor(hot[slot], iota_rep[:, 0:columns, :],
                                             v.to_broadcast([P, columns, HK]), ALU.is_equal)

                at_least(dve, token_ok, h - 1)
                equal(tile_hot, slot_tile, RT).then_inc(tile_ok, 1)
                at_least(dve, hot_used, h - 1)
                equal(row_hot, slot_row, P).then_inc(row_ok, 1)

            hot_steps(hots)
            then(dve.tensor_scalar(te_cmp[:, :], first_tile[:, :], part_f[:, :], None, ALU.is_le))
            then(dve.tensor_reduce(te_col[:, :], te_cmp[:, :], AX.X, ALU.add))
            dve.tensor_scalar(te_col[:, :], te_col[:, :], -1.0, None, ALU.add).then_inc(te_ok, 1)
            dve.wait_ge(hot_used, NT // HT)
            dve.tensor_copy(token_of[:, 0:RT], bank[2][:, 0:RT]).then_inc(slots_ok, 1)
            dve.wait_ge(te_ps, 1)
            dve.tensor_copy(tile_expert[0:1, G * DEPTH:G * DEPTH + RT], bank[3][0:1, 0:RT]).then_inc(route_ok, 1)

            for k in range(K):
                then(dve.tensor_tensor(r2, r1, top_v[:, :, k:k + 1].to_broadcast([P, NT, E]), ALU.is_equal))
                then(dve.tensor_tensor(r3, r2, score, ALU.mult))
                ins = dve.tensor_reduce(prob[:, k, :], r3, AX.X, ALU.add)
            then(ins)
            then(dve.tensor_reduce(prob_sum[:, :], prob[:, :, :].rearrange("p k t -> p t k"), AX.X, ALU.add))
            then(dve.tensor_scalar(prob_sum[:, :], prob_sum[:, :], 1e-20, SPLIT * SPLIT, ALU.add, ALU.mult))
            then(dve.reciprocal(prob_sum[:, :], prob_sum[:, :]))
            dve.tensor_tensor(weight[:, :, :], prob[:, :, :].rearrange("p k t -> p t k"),
                                   prob_sum[:, :].rearrange("p (t a) -> p t a", a=1).to_broadcast([P, NT, K]),
                                   ALU.mult).then_inc(weight_ok, 1)

            dve.wait_ge(gateb_ld, 16 * B)

            def group(i):
                for q in range(STEPS):
                    if (now := pair(i, q, 2)) is not None:
                        j, slot, place, body = now
                        dve.wait_ge(silu_ok, j + 1)
                        dve.tensor_tensor(hid[:, slot, :, :], act_g[:, slot, :, :], clip[:, slot, :, I:2 * I],
                                          ALU.mult).then_inc(hid_ok, 1)
                    if (now := pair(i, q, 4)) is not None:
                        j, slot, place, body = now
                        products = bank[6 + slot][:, 0:G * D].rearrange("p (g n) -> p g n", g=G)
                        dve.wait_ge(y_ps, j + 1)
                        if not shared(i, j):
                            at_least(dve, y_stored[slot], 16 * (STEPS // 2 * body + place // 2))
                            dve.tensor_copy(yo[:, slot, :, :], products).then_inc(y_ok, 1)
                        else:
                            b = j - RT // G
                            if b < 2:
                                dve.wait_ge(y_stored[slot], 16 * (j // 2))
                            else:
                                dve.wait_ge(shx_ok, b - 1)
                            dve.scalar_tensor_tensor(yo[:, slot, :, :], products, 1.0 / (SPLIT * SPLIT),
                                                     gate_b[:, b:b + 1, :].to_broadcast([P, G, D]),
                                                     ALU.mult, ALU.mult).then_inc(shy_ok, 1)
                    if (now := pair(i, q, 3)) is not None:
                        j, slot, place, body = now
                        dve.wait_ge(hidhi_ok, j + 1)
                        dve.tensor_tensor(hidT[:, slot, 1, :, :].rearrange("p g n -> p (g n)"),
                                          bank[4 + slot][:, 0:G * P],
                                          hidT[:, slot, 0, :, :].rearrange("p g n -> p (g n)"),
                                          ALU.subtract).then_inc(hidlo_ok, 1)
                    if (now := pair(i, q, 1)) is not None:
                        j, slot, place, body = now
                        dve.wait_ge(gu_ps, j + 1)
                        dve.tensor_scalar(clip[:, slot, :, :].rearrange("p g n -> p (g n)"), bank[2 + slot][:, :],
                                          CLAMP * SPLIT, -CLAMP * SPLIT, ALU.min, ALU.max).then_inc(clip_ok, 1)
                    now = pair(i, q, 4)
                    if now is not None and shared(i, now[0]):
                        j, slot, place, body = now
                        b = j - RT // G
                        dve.wait_ge(shy_ok, b + 1)
                        dve.tensor_tensor(xs[:, G * b:G * b + G, :], xs[:, G * b:G * b + G, :], yo[:, slot, :, :],
                                          ALU.add).then_inc(shx_ok, 1)

            pair_steps(dve, group)

            dve.wait_ge(shx_ok, NT // G)
            dve.wait_ge(weight_ok, 1)

            def comb(i):
                for u in range(CU):
                    t = CU * i + u
                    steps_t = CS * CU * i + CS * u
                    w = weight[:, ds(t, 1), :].rearrange("p a k -> p (a k)")
                    gate = gate_b[:, ds(CU // TPB * i + u // TPB, 1), :].rearrange("p a d -> p (a d)")
                    a = [acc[:, 2 * u + n % 2, :] for n in range(K + 1)]
                    dve.wait_ge(first_ok, t + 1)
                    total = fin[:, ds(t, 1), :].rearrange("p a d -> p (a d)")
                    for k in range(1, K):
                        if k > 1:
                            dve.wait_ge(comb_step, steps_t + k - 1)
                        dve.scalar_tensor_tensor(a[k], yg[:, u, k, :], w[:, k:k + 1], total if k == 1 else a[k - 1],
                                                 ALU.mult, ALU.add).then_inc(comb_step, 1)
                    dve.wait_ge(comb_step, steps_t + K - 1)
                    dve.tensor_tensor(a[K], a[K - 1], gate, ALU.mult).then_inc(comb_step, 1)
                    dve.wait_ge(comb_step, steps_t + K)
                    dve.tensor_tensor(total, a[K], xs[:, ds(t, 1), :].rearrange("p a d -> p (a d)"),
                                      ALU.add).then_inc(fin_ok, 1)

            with dve.Fori(0, NT // CU) as i:
                comb(i)

        @block.tensor
        def _(pe):
            pe.wait_ge(consts, 10)
            pe.wait_ge(c_act, 1)
            for c in range(C):
                ins = pe.transpose(bank[0][:, c * B:(c + 1) * B], c_s[:, c * P:(c + 1) * P], ident[0:B, 0:B])
            ins.then_inc(cT_ps, 1)
            pe.wait_ge(keep_ok, 1)
            pe.transpose(bank[3][:, 0:C], dec[:, :], ident[0:C, 0:C]).then_inc(dec_ps, 1)
            pe.wait_ge(cT_ok, 1)
            pe.wait_ge(ld_wmod, 16)
            for n in (1, 2):
                for c in range(C):
                    ins = pe.matmul(bank[n][0:B, :], cT[:, c, :], wmod_s[:, c, n * 512:(n + 1) * 512],
                                    start=(c == 0), stop=(c == C - 1))
            ins.then_inc(mod_ps, 1)
            pe.wait_ge(keep_ok, 1 + C)
            for n in range(2 * C):
                for c in range(C):
                    ins = pe.matmul(bank[3][:, 64 + n * B:64 + (n + 1) * B], wmod_s[:, c, n * P:(n + 1) * P],
                                    cT[:, c, :], start=(c == 0), stop=(c == C - 1))
            ins.then_inc(modT_ps, 1)
            for w, src in enumerate((wa_k[:, :, :], wa_n[:, 1, :, :])):
                for c in range(C):
                    for e in range(C):
                        ins = pe.transpose(bank[(7, 4)[w]][:, c * D + e * P:c * D + (e + 1) * P],
                                           src[:, e, c * P:(c + 1) * P], ident[:, :])
                ins.then_inc(w_ps, 1)
            pe.wait_ge(ld_small, 48)
            for c in range(C):
                pe.transpose(bank[6][:, D + c * E:D + (c + 1) * E], rt_n[:, c * P:(c + 1) * P], ident[0:E, 0:E])
            pe.wait_ge(ld_shared, 48)
            for r in range(C):
                ins = pe.transpose(bank[6][:, r * P:(r + 1) * P], nat_sh[:, 2, r * I:(r + 1) * I], ident[:, :])
            ins.then_inc(w_ps, 1)
            for c in range(C):
                for m in range(2):
                    ins = pe.transpose(bank[5][:, (2 * c + m) * P:(2 * c + m + 1) * P],
                                       nat_sh[:, m, c * P:(c + 1) * P], ident[:, :])
            ins.then_inc(w_ps, 1)
            pe.wait_ge(wa_ok, 2)

            def transposes(s, units):
                for u in units:
                    h, j = u // 3, u % 3
                    pe.wait_ge(nat_ld[h], 64 * s + 64)
                    if isinstance(s, int) and s == 0 and u == 0:
                        pe.wait_ge(w_lo, 3)
                    at_least(pe, pair_lo, UNITS * s + u - 2)
                    if j < 2:
                        for c in range(C):
                            for m in range(2):
                                ins = pe.transpose(bank[5 + j][:, (2 * c + m) * P:(2 * c + m + 1) * P],
                                                   nat[:, h, m, j, c * P:(c + 1) * P], ident[:, :])
                    else:
                        for e in range(2):
                            for r in range(C):
                                ins = pe.transpose(bank[7][:, e * D + r * P:e * D + (r + 1) * P],
                                                   nat[:, h, 2, e, r * I:(r + 1) * I], ident[:, :])
                    ins.then_inc(pair_ps, 1)

            def body(s):
                if batch(s):
                    pe.wait_ge(xh_ok, s + 1)
                    for q in range(TPB):
                        for c in range(C):
                            ins = pe.transpose(bank[0][:, c * S + q * P:c * S + (q + 1) * P],
                                               xh[:, q, c * P:(c + 1) * P], ident[:, :])
                    ins.then_inc(xhT_ps, 1)
                if batch(s - 3):
                    pe.wait_ge(h16lo_ok, s - 2)
                    for q in range(TPB):
                        for n in range(2 * C):
                            ins = pe.transpose(bank16[3][:, (q * 2 * C + n) * P:(q * 2 * C + n + 1) * P],
                                               h16[:, q, n * P:(n + 1) * P], ident16[:, :])
                    ins.then_inc(h16T_ps, 1)
                if batch(s):
                    transposes(s, (0, 1))
                if batch(s - 1):
                    pe.wait_ge(state_ok, s)
                    for q in range(TPB):
                        for c in range(C):
                            ins = pe.matmul(bank[2][:, q * D:(q + 1) * D], st[:, c, q * P:(q + 1) * P],
                                            wa_T[:, 1, c, :], start=(c == 0), stop=(c == C - 1))
                    ins.then_inc(attn_ps, 1)
                if batch(s):
                    transposes(s, (2,))
                    pe.wait_ge(hT_ok, s + 1)
                    if isinstance(s, int) and s == 0:
                        pe.wait_ge(rows_ok, 1)
                    for e in range(C):
                        for c in range(C):
                            ins = pe.matmul(bank[1][:, e * S:(e + 1) * S], wa_T[:, 0, c, e * P:(e + 1) * P],
                                            hT[:, c, :], start=(c == 0), stop=(c == C - 1))
                    ins.then_inc(proj_ps, 1)
                    transposes(s, range(3, UNITS - 1))
                if batch(s - 3):
                    pe.wait_ge(h16T_ok, s - 2)
                    for q in range(TPB):
                        for n, (c, (a, m)) in enumerate((c, p) for c in range(C) for p in PARTS):
                            ins = pe.matmul(bank[4][:, q * E:(q + 1) * E], h16T[:, q, a * C + c, :],
                                            rt_T[:, c, m, :], start=(n == 0), stop=(n == 3 * C - 1))
                    ins.then_inc(logit_ps, 1)
                if batch(s):
                    transposes(s, (UNITS - 1,))

            mixer_steps(pe, body)

            def count(t):
                return pe.matmul(bank[1][:, 0:E], ones16[:, :], picked[:, t, :], start=(t == 0), stop=(t == NT - 1))

            def before(c):
                return pe.matmul(bank[0][:, c.start * E:c.stop * E], before16[:, :],
                                 picked[:, c, :].rearrange("p t e -> p (t e)"),
                                 start=(c.start == 0), stop=False)

            def earlier(t, first=None, last=NT - 1):
                first = t + 1 if first is None else first
                return pe.matmul(bank[0][:, first * E:(last + 1) * E].rearrange("p (t e) -> p t e", e=E),
                                 ones16[:, :], picked[:, t:t + 1, :].to_broadcast([P, last + 1 - first, E]),
                                 start=False, stop=(t == NT - 2))

            pe.wait_ge(r_picked, 1)
            for t in range(SPLIT_AT):
                count(t)
            before(SCORED[0])
            earlier(0, 1, SPLIT_AT - 1)
            earlier(0, SPLIT_AT)
            for t in range(1, SPLIT_AT):
                earlier(t)
            pe.wait_ge(r_picked, 2)
            for t in range(SPLIT_AT, NT):
                ins = count(t)
            ins.then_inc(count_ps, 1)
            before(SCORED[1])
            for t in range(SPLIT_AT, NT - 1):
                ins = earlier(t)
            ins.then_inc(rank_ps, 1)

            def slots(h, slot, first, last):
                pe.wait_ge(row_ok, h + 1)
                pe.wait_ge(token_ok, h + 1)
                for m in range(HK):
                    ins = pe.matmul(bank[2][:, 0:RT], row_hot[slot][:, :, m], tile_token[slot][:, :, m],
                                    start=(first and m == 0), stop=(last and m == HK - 1))
                ins.then_inc(hot_used, 1)

            hot_steps(slots)
            pe.wait_ge(te_ok, 1)
            pe.matmul(bank[3][0:1, 0:P], te_col[:, :], ident[:, :], start=True, stop=True).then_inc(te_ps, 1)
            pe.wait_ge(slots_ok, 1)
            pe.wait_ge(route_ok, 1)

            HALF = U // 2
            regs = [[pe.alloc_register(f"tile_expert{h}_{n}") for n in range(U + G)] for h in range(2)]

            def load_experts(h, i):
                pe.load(regs[h], tile_expert[0:1, ds(U * i + HALF * h, U + G)])

            load_experts(0, 0)

            def group(i):
                expert = {n: pe.snap(r, min_val=0, max_val=E) for n, r in enumerate(regs[0])}
                for q in range(STEPS):
                    if (now := pair(i, q, 0)) is not None:
                        j, slot, place, body = now
                        if not shared(i, j):
                            pe.wait_ge(gathered[place], 16 * G * body + 16 * G)
                        else:
                            pe.wait_ge(sh_rows[place], 16 * (body - RT // U) + 16)
                        for g in range(G):
                            for n in range(2 * C):
                                m = g * 2 * C + n
                                ins = pe.transpose(bank16[slot][:, m * P:(m + 1) * P],
                                                   xg[:, place, g, n * P:(n + 1) * P], ident16[:, :])
                        ins.then_inc(xT_ps, 1)
                    if (now := pair(i, q, 4)) is not None:
                        j, slot, place, body = now
                        pe.wait_ge(hidlo_ok, j + 1)
                        for g in range(G):
                            w = wdn[:, ds(expert[G * q + g], 1), :, :].rearrange("p a h d -> p (a h) d")
                            for n, (a, m) in enumerate(PARTS):
                                ins = pe.matmul(bank[6 + slot][:, g * D:(g + 1) * D], hidT[:, slot, a, g, :],
                                                w[:, m, :], start=(n == 0), stop=(n == 2))
                        ins.then_inc(y_ps, 1)
                    if (now := pair(i, q, 3)) is not None:
                        j, slot, place, body = now
                        pe.wait_ge(hid_ok, j + 1)
                        for g in range(G):
                            ins = pe.transpose(bank[4 + slot][:, g * P:(g + 1) * P], hid[:, slot, g, :], ident[:, :])
                        ins.then_inc(hidT_ps, 1)
                    if (now := pair(i, q, 1)) is not None:
                        j, slot, place, body = now
                        pe.wait_ge(xT_ok, j + 1)
                        for g in range(G):
                            w = wgu[:, ds(expert[U + G * (q - 1) + g], 1), :, :, :]\
                                .rearrange("p a c h n -> p (a c) h n")
                            for n, (c, (a, m)) in enumerate((c, p) for c in range(C) for p in PARTS):
                                ins = pe.matmul(bank[2 + slot][:, g * 2 * I:(g + 1) * 2 * I],
                                                xT[:, slot, g, a * C + c, :], w[:, c, m, :],
                                                start=(n == 0), stop=(n == 3 * C - 1))
                        ins.then_inc(gu_ps, 1)
                    if q == 0:
                        load_experts(1, i)
                    if q == STEPS // 2:
                        load_experts(0, i + 1)
                    if q == STEPS // 2 - 1:
                        expert = {HALF + n: pe.snap(r, min_val=0, max_val=E) for n, r in enumerate(regs[1])}

            pair_steps(pe, group)


_INS = ["L0_attn_x", "L0_attn_W_in", "L0_attn_W_out", "L0_attn_decay", "L0_attn_bias",
        "L0_ffn_router_w", "L0_ffn_expert_bias", "L0_ffn_gate_w", "L0_ffn_up_w", "L0_ffn_down_w",
        "L0_ffn_shared_gate_w", "L0_ffn_shared_up_w", "L0_ffn_shared_down_w", "L0_c", "L0_wmod"]


def kernel(**inputs):
    import numpy as _np
    import concourse.bacc as _bacc
    from concourse import mybir as _mybir
    from concourse.bass_utils import run_bass_kernel_spmd as _run

    nc = _bacc.Bacc("TRN2", target_bir_lowering=False, num_devices=1)
    arrays, args = {}, []
    for name in _INS:
        a = _np.ascontiguousarray(inputs[name])
        arrays[f"in_{name}_dram"] = a
        args.append(nc.dram_tensor(f"in_{name}_dram", a.shape, _mybir.dt.from_np(a.dtype), kind="ExternalInput").ap())
    o = nc.dram_tensor("out_0_dram", inputs["L0_attn_x"].shape, _mybir.dt.float32, kind="ExternalOutput").ap()
    adaln_block(nc, *args, o)
    r = _run(nc, [arrays], core_ids=[0])
    return r.results[0]["out_0_dram"]
```
